# Optimizing a Trainium2 kernel written in Bass

```python
import numpy as np
import jax
import jax.numpy as jnp

def _softmax(x, axis=-1):
    return jax.nn.softmax(x, axis=axis)

def _gelu(x):
    return jax.nn.gelu(x, approximate=True)

def _silu(x):
    return jax.nn.silu(x)

def _sigmoid(x):
    return jax.nn.sigmoid(x)

def _layernorm(x, axis=-1, eps=1e-05):
    m = jnp.mean(x, axis=axis, keepdims=True)
    v = jnp.var(x, axis=axis, keepdims=True)
    return (x - m) / jnp.sqrt(v + eps)

def _scatter_add(tgt, idx, src, axis=0):
    return tgt.at[idx].add(src)

def _segment_sum(src, seg, n):
    return jax.ops.segment_sum(src, seg, n)
kernel_name = 'mk_early_fusion_d1_tok_img1024_r4_9833e4'

def setup_inputs(seed: int=0):
    np.random.seed(seed)
    _w = jnp.asarray

    def _rec_inputs():
        import jax
        import jax.numpy as jnp
        _rk = jax.random.key(seed)
        x = -0.00016672 + 0.999947 * jax.random.normal(jax.random.fold_in(_rk, 1), (32, 3, 96, 96), jnp.float32)
        txt = -6.04713e-11 + 0.999984 * jax.random.normal(jax.random.fold_in(_rk, 2), (32, 32, 256), jnp.float32)
        return (x, txt)
    x, txt = _rec_inputs()

    def _L0_tok_setup():
        import jax, jax.numpy as jnp
        import numpy as np
        PATCH = 16
        EPS = 1e-05

        def _patchify(x, p):
            B, C, H, W = x.shape
            hp, wp = (H // p, W // p)
            x = x.reshape(B, C, hp, p, wp, p)
            x = x.transpose(0, 2, 4, 1, 3, 5)
            return x.reshape(B, hp * wp, C * p * p)
        key = jax.random.key(seed)
        ks = jax.random.split(key, 6)
        B, C, H = (64, 3, 96)
        E = 256
        P = PATCH
        N = (H // P) ** 2
        D = C * P * P
        x = jax.random.normal(ks[0], (B, C, H, H), dtype=jnp.float32)
        W = jax.random.normal(ks[1], (D, E), dtype=jnp.float32) * (1.0 / np.sqrt(D))
        b = jnp.zeros((E,), dtype=jnp.float32)
        cls_token = jax.random.normal(ks[2], (1, 1, E), dtype=jnp.float32) * 0.02
        pos_embedding = jax.random.normal(ks[3], (1, N + 1, E), dtype=jnp.float32) * 0.02
        gamma = jnp.ones((E,), dtype=jnp.float32)
        beta = jnp.zeros((E,), dtype=jnp.float32)
        return {'x': x, 'W': W, 'b': b, 'cls_token': cls_token, 'pos_embedding': pos_embedding, 'gamma': gamma, 'beta': beta}
    _L0_tok_all = _L0_tok_setup()
    _L0_tok_in = {k: v for k, v in _L0_tok_all.items() if k in ('W', 'b', 'cls_token', 'pos_embedding', 'gamma', 'beta')}
    del _L0_tok_all

    def _L0_attn_setup():
        import jax, jax.numpy as jnp
        import numpy as np
        import math
        NUM_BUCKETS = 32
        MAX_DISTANCE = 128
        N_HEADS = 16
        D_KV = 64

        def _relative_position_bucket(relative_position, num_buckets=NUM_BUCKETS, max_distance=MAX_DISTANCE):
            nb = num_buckets // 2
            rel_buckets = (relative_position > 0).astype(jnp.int32) * nb
            rp = jnp.abs(relative_position)
            max_exact = nb // 2
            is_small = rp < max_exact
            rp_large = max_exact + (jnp.log(rp.astype(jnp.float32) / max_exact) / math.log(max_distance / max_exact) * (nb - max_exact)).astype(jnp.int32)
            rp_large = jnp.minimum(rp_large, nb - 1)
            return rel_buckets + jnp.where(is_small, rp, rp_large)

        def compute_position_bias(rel_bias_table, q_len, k_len):
            ctx = jnp.arange(q_len, dtype=jnp.int32)[:, None]
            mem = jnp.arange(k_len, dtype=jnp.int32)[None, :]
            buckets = _relative_position_bucket(mem - ctx)
            values = rel_bias_table[buckets]
            return jnp.transpose(values, (2, 0, 1))[None]
        key = jax.random.key(seed)
        ks = jax.random.split(key, 6)
        B, S, D = (2, 512, 256)
        s = 0.02
        return {'hidden_states': jax.random.normal(ks[0], (B, S, D), dtype=jnp.float32), 'Wq': jax.random.normal(ks[1], (D, N_HEADS * D_KV), dtype=jnp.float32) * s, 'Wk': jax.random.normal(ks[2], (D, N_HEADS * D_KV), dtype=jnp.float32) * s, 'Wv': jax.random.normal(ks[3], (D, N_HEADS * D_KV), dtype=jnp.float32) * s, 'Wo': jax.random.normal(ks[4], (N_HEADS * D_KV, D), dtype=jnp.float32) * s, 'rel_bias_table': jax.random.normal(ks[5], (NUM_BUCKETS, N_HEADS), dtype=jnp.float32)}
    _L0_attn_all = _L0_attn_setup()
    _L0_attn_in = {k: v for k, v in _L0_attn_all.items() if k in ('Wq', 'Wk', 'Wv', 'Wo', 'rel_bias_table')}
    del _L0_attn_all

    def _L0_ffn_setup():
        import jax, jax.numpy as jnp
        import numpy as np
        B, N, D, E, R, K = (4, 512, 256, 8, 64, 2)
        key = jax.random.key(seed)
        ks = jax.random.split(key, 5)
        scale = 0.02
        return {'x': jax.random.normal(ks[0], (B, N, D), dtype=jnp.float32), 'gate_w': jax.random.normal(ks[1], (D, E), dtype=jnp.float32) * scale, 'Wu': jax.random.normal(ks[2], (E, D, R), dtype=jnp.float32) * scale, 'Wv': jax.random.normal(ks[3], (E, D, R), dtype=jnp.float32) * scale, 'Wo': jax.random.normal(ks[4], (E, R, D), dtype=jnp.float32) * scale}
    _L0_ffn_all = _L0_ffn_setup()
    _L0_ffn_in = {k: v for k, v in _L0_ffn_all.items() if k in ('gate_w', 'Wu', 'Wv', 'Wo')}
    del _L0_ffn_all
    return {'x': x, 'txt': txt, 'L0_tok_W': _L0_tok_in['W'], 'L0_tok_b': _L0_tok_in['b'], 'L0_tok_cls_token': _L0_tok_in['cls_token'], 'L0_tok_pos_embedding': _L0_tok_in['pos_embedding'], 'L0_tok_gamma': _L0_tok_in['gamma'], 'L0_tok_beta': _L0_tok_in['beta'], 'L0_attn_Wq': _L0_attn_in['Wq'], 'L0_attn_Wk': _L0_attn_in['Wk'], 'L0_attn_Wv': _L0_attn_in['Wv'], 'L0_attn_Wo': _L0_attn_in['Wo'], 'L0_attn_rel_bias_table': _L0_attn_in['rel_bias_table'], 'L0_ffn_gate_w': _L0_ffn_in['gate_w'], 'L0_ffn_Wu': _L0_ffn_in['Wu'], 'L0_ffn_Wv': _L0_ffn_in['Wv'], 'L0_ffn_Wo': _L0_ffn_in['Wo']}

def reference(x, txt, L0_tok_W, L0_tok_b, L0_tok_cls_token, L0_tok_pos_embedding, L0_tok_gamma, L0_tok_beta, L0_attn_Wq, L0_attn_Wk, L0_attn_Wv, L0_attn_Wo, L0_attn_rel_bias_table, L0_ffn_gate_w, L0_ffn_Wu, L0_ffn_Wv, L0_ffn_Wo):
    import jax
    import jax.numpy as jnp

    def _L0_tok_ref(x, W, b, cls_token, pos_embedding, gamma, beta):
        import jax, jax.numpy as jnp
        import numpy as np
        PATCH = 16
        EPS = 1e-05

        def _patchify(x, p):
            B, C, H, W = x.shape
            hp, wp = (H // p, W // p)
            x = x.reshape(B, C, hp, p, wp, p)
            x = x.transpose(0, 2, 4, 1, 3, 5)
            return x.reshape(B, hp * wp, C * p * p)
        B = x.shape[0]
        patches = _patchify(x, PATCH)
        tok = jnp.einsum('bnd,de->bne', patches, W) + b
        cls = jnp.broadcast_to(cls_token, (B, 1, tok.shape[-1]))
        h = jnp.concatenate([cls, tok], axis=1) + pos_embedding
        mu = jnp.mean(h, axis=-1, keepdims=True)
        var = jnp.mean(jnp.square(h - mu), axis=-1, keepdims=True)
        out = (h - mu) * jax.lax.rsqrt(var + EPS) * gamma + beta
        return out

    def _L0_attn_ref(hidden_states, Wq, Wk, Wv, Wo, rel_bias_table):
        import jax, jax.numpy as jnp
        import numpy as np
        import math
        NUM_BUCKETS = 32
        MAX_DISTANCE = 128
        N_HEADS = 16
        D_KV = 64

        def _relative_position_bucket(relative_position, num_buckets=NUM_BUCKETS, max_distance=MAX_DISTANCE):
            nb = num_buckets // 2
            rel_buckets = (relative_position > 0).astype(jnp.int32) * nb
            rp = jnp.abs(relative_position)
            max_exact = nb // 2
            is_small = rp < max_exact
            rp_large = max_exact + (jnp.log(rp.astype(jnp.float32) / max_exact) / math.log(max_distance / max_exact) * (nb - max_exact)).astype(jnp.int32)
            rp_large = jnp.minimum(rp_large, nb - 1)
            return rel_buckets + jnp.where(is_small, rp, rp_large)

        def compute_position_bias(rel_bias_table, q_len, k_len):
            ctx = jnp.arange(q_len, dtype=jnp.int32)[:, None]
            mem = jnp.arange(k_len, dtype=jnp.int32)[None, :]
            buckets = _relative_position_bucket(mem - ctx)
            values = rel_bias_table[buckets]
            return jnp.transpose(values, (2, 0, 1))[None]
        B, S, D = hidden_states.shape
        H, dh = (N_HEADS, D_KV)
        q = (hidden_states @ Wq).reshape(B, S, H, dh)
        k = (hidden_states @ Wk).reshape(B, S, H, dh)
        v = (hidden_states @ Wv).reshape(B, S, H, dh)
        position_bias = compute_position_bias(rel_bias_table, S, S)
        scale = 1.0 / math.sqrt(dh)
        scores = jnp.einsum('bqhd,bkhd->bhqk', q, k) * scale + position_bias
        probs = jax.nn.softmax(scores, axis=-1)
        ctx = jnp.einsum('bhqk,bkhd->bqhd', probs, v).reshape(B, S, H * dh)
        attn_output = ctx @ Wo
        return attn_output

    def _L0_ffn_ref(x, gate_w, Wu, Wv, Wo):
        import jax, jax.numpy as jnp
        import numpy as np
        B, N, D, E, R, K = (4, 512, 256, 8, 64, 2)
        logits = jnp.einsum('bnd,de->bne', x, gate_w)
        topv, topi = jax.lax.top_k(logits, K)
        w = jax.nn.softmax(topv, axis=-1)
        u = jnp.einsum('bnd,edr->bner', x, Wu)
        v = jnp.einsum('bnd,edr->bner', x, Wv)
        s = jax.nn.silu(u) * v
        Y = jnp.einsum('bner,erd->bned', s, Wo)
        y_sel = jnp.take_along_axis(Y, topi[..., None], axis=2)
        out = jnp.einsum('bnkd,bnk->bnd', y_sel, w)
        return out
    h = _L0_tok_ref(x, L0_tok_W, L0_tok_b, L0_tok_cls_token, L0_tok_pos_embedding, L0_tok_gamma, L0_tok_beta)
    h = jnp.concatenate([h, txt], axis=1)
    h = h + _L0_attn_ref(_layernorm(h, axis=-1), L0_attn_Wq, L0_attn_Wk, L0_attn_Wv, L0_attn_Wo, L0_attn_rel_bias_table)
    h = h + _L0_ffn_ref(_layernorm(h, axis=-1), L0_ffn_gate_w, L0_ffn_Wu, L0_ffn_Wv, L0_ffn_Wo)
    return h

_drawn_inputs = setup_inputs


def setup_inputs(seed=0):
    import zlib

    import numpy as np

    out = dict(_drawn_inputs(seed))
    spreads = {'L0_tok_b': (0.0, 0.1), 'L0_tok_gamma': (1.0, 0.2), 'L0_tok_beta': (0.0, 0.1)}
    factors = {'L0_attn_Wq': 8.0,
     'L0_attn_Wk': 8.0,
     'L0_ffn_gate_w': 8.0,
     'L0_ffn_Wu': 8.0,
     'L0_ffn_Wv': 8.0,
     'L0_ffn_Wo': 8.0}
    for name, (base, spread) in spreads.items():
        noise = np.random.default_rng([zlib.crc32(name.encode()), seed]).standard_normal(out[name].shape)
        drawn = base * np.exp(spread * noise) if base else spread * noise
        out[name] = jnp.asarray(drawn.astype(out[name].dtype))
    for name, factor in factors.items():
        out[name] = (out[name] * factor).astype(out[name].dtype)
    return out
```

```python
from contextlib import ExitStack

import numpy as np

import concourse.bass as bass
from concourse import mybir

F32 = mybir.dt.float32
F32R = mybir.dt.float32r
ALU = mybir.AluOpType
ACT = mybir.ActivationFunctionType
AX = mybir.AxisListType

P = 128
BATCH, CHAN, IMG, PATCH = 32, 3, 96, 16
SIDE = IMG // PATCH
NPATCH = SIDE * SIDE
NTOK = NPATCH + 1
NTXT = 32
S = NTOK + NTXT
SP = S + 1
D = 256
KD = D // P
PDIM = CHAN * PATCH * PATCH
KT = PDIM // P
HEADS, DH = 16, 64
PAIRS = HEADS // 2
GB = 4
GROUPS = BATCH // GB
COLS = GB * SP
PCOLS = GB * NPATCH
E, R = 8, 64
FT = E * R // P
SLOTS = 2 * PAIRS
NREL = 2 * S - 1
BUCKETS = 32
EPS = 1e-5
SCALE = DH ** -0.5
PIECE = 768
TOP2_STEPS = 11


def fillers(n):
    return {
        1: [("B", "wo", 0)],
        2: [("B", "wo", 1)],
        3: [("B", "aback", 0), ("B", "aback", 1), ("F", "tok", 0)],
        4: [("F", "tok", 1)],
        5: [("F", "tback", 0), ("F", "tback", 1)],
        6: [("B", "xb", 0), ("B", "xb", 1)],
        7: [("B", "logit", 0), ("B", "u", 0), ("B", "v", 0)],
        8: [("B", "u", 1), ("B", "v", 1)],
        9: [("B", "u", 2), ("B", "v", 2)],
        10: [("B", "u", 3), ("B", "v", 3), ("B", "wT", 0)],
        11: [("B", "mix", 0), ("B", "mix", 1), ("B", "mix", 2), ("B", "mix", 3)],
        12: [("F", "xf", 0), ("F", "xf", 1), ("B", "down", 0)],
        13: [("B", "down", 1)],
        14: [("B", "yback", 0), ("B", "yback", 1)],
    }.get(n, [])


def projections(n):
    if n % 2 == 0:
        return [("q", n // 2 + 2), ("k", n // 2 + 2)]
    return [("vback", (n + 1) // 2), ("vT", (n + 3) // 2)]


def exists(g, off):
    return not isinstance(g, int) or 0 <= g + off < GROUPS


def slot_jobs(g, n):
    off = {"F": 1, "B": -1}
    fill = [(k, i) for side, k, i in fillers(n) if exists(g, off[side])]
    proj = [(k, p) for k, p in projections(n) if exists(g, p // PAIRS)]
    return fill, proj


def body_jobs(g):
    return [j for n in range(SLOTS) for part in slot_jobs(g, n) for j in part]


SIDED = ("tok", "xf", "xb", "q", "k", "vback", "logit", "wT")
LOOP_FROM, LOOP_TO = 1, GROUPS - 1
BODY_LIST = {g: body_jobs(g) for g in range(-1, GROUPS + 1)}
BODY_BASE = {g: sum(len(BODY_LIST[b]) for b in range(-1, g)) for g in range(-1, GROUPS + 1)}
PER_BODY = len(BODY_LIST[LOOP_FROM])
SIDED_BASE = {g: sum(k in SIDED for b in range(-1, g) for k, _ in BODY_LIST[b]) for g in range(-1, GROUPS + 1)}
SIDED_PER_BODY = sum(k in SIDED for k, _ in BODY_LIST[LOOP_FROM])
assert PER_BODY % 2 == 0


class Job:

    def __init__(self, g, kind, i, off=0):
        if isinstance(g, int):
            body, g = g + off, 0
            at = BODY_LIST[body].index((kind, i))
            number, sided = BODY_BASE[body] + at, SIDED_BASE[body]
        else:
            body, back = LOOP_FROM, LOOP_FROM - off
            at = BODY_LIST[body].index((kind, i))
            number, sided = BODY_BASE[body] + at - PER_BODY * back, SIDED_BASE[body] - SIDED_PER_BODY * back
        sided += sum(k in SIDED for k, _ in BODY_LIST[body][:at + 1])
        self.bank = number % 2
        self.number = g * PER_BODY + number
        self.before = g * (PER_BODY // 2) + number // 2
        self.sided = g * SIDED_PER_BODY + sided


def projected(g, kind, p):
    early = p < (1 if kind == "vback" else 2)
    return Job(g, kind, p + PAIRS, -1) if early else Job(g, kind, p)


def alive(g, m):
    return not isinstance(g, int) or 0 <= SLOTS * g + m < SLOTS * GROUPS


def at_least(eng, semaphore, value):
    if not isinstance(value, int) or value > 0:
        eng.wait_ge(semaphore, value)


def build(nc, xp, txt, wtok, btok, cls, pos, gamma, beta, wqkv, wo, table, gatew, wup, wdown, onehot, out):
    with ExitStack() as ctx:
        def sb(name, shape, dt=F32):
            return ctx.enter_context(nc.sbuf_tensor(name, shape, dt))

        def pb(name):
            return ctx.enter_context(nc.psum_tensor(name, [P, 2, 512], F32))

        def sem(name):
            return ctx.enter_context(nc.semaphore(name))

        def pair_of(name, shape):
            return [sb(f"{name}_hi", shape, F32R), sb(f"{name}_lo", shape, F32R)]

        Wtok = pair_of("Wtok", [P, KT, D])
        Wqkv = pair_of("Wqkv", [P, PAIRS, 3, KD, P])
        Wo = pair_of("Wo", [P, PAIRS, D])
        Wup = pair_of("Wup", [P, FT, 2, KD, P])
        Wdown = pair_of("Wdown", [P, FT, D])
        Wgate = sb("Wgate", [P, KD, 2, E], F32R)
        stage = sb("stage", [P, 2, PIECE])
        ident = sb("ident", [P, P])
        select = sb("select", [E, FT, P], F32R)
        earlier = sb("earlier", [P, E, E])
        minus_half = sb("minus_half", [P, GB])
        posb = sb("posb", [NTOK, D])
        gammab = sb("gammab", [NTOK, D])
        betab = sb("betab", [NTOK, D])
        gate_f = sb("gate_f", [P, KD, E])
        bias = sb("bias", [S, HEADS, S])
        x_raw = sb("x_raw", [P, KT, PCOLS])
        x_pix = sb("x_pix", [P, KT, 2, PCOLS], F32R)
        tok_a = sb("tok_a", [P, PCOLS])
        tokT = sb("tokT", [P, KD, GB * NTOK + NTXT])
        h_new = sb("h_new", [S, GB, D])
        h_mid = sb("h_mid", [S, GB, D])
        h_res = sb("h_res", [S, GB, D])
        xn = sb("xn", [S, GB, D])
        XT = pair_of("XT", [P, KD, GB, SP])
        XB = pair_of("XB", [P, KD, GB, SP])
        ln = {k: dict(st=sb(f"st_{k}", [S, GB, 6]), mv=sb(f"mv_{k}", [S, GB, 2]), ve=sb(f"ve_{k}", [S, GB]),
                      rs=sb(f"rs_{k}", [S, GB]), nm=sb(f"nm_{k}", [S, GB])) for k in ("tok", "front", "back")}
        Q = [pair_of(f"Q{i}", [P, GB, SP]) for i in range(2)]
        K = [sb(f"K{i}", [P, GB, 2, SP], F32R) for i in range(2)]
        vT = sb("vT", [P, GB, SP])
        V = [pair_of(f"V{i}", [S, GB, P]) for i in range(2)]
        prob = sb("prob", [S, 4, 4, S])
        mx = sb("mx", [S, 2, 4])
        sm = sb("sm", [S, 2, 4])
        rc = sb("rc", [S, 2, 4])
        PT = [sb(f"PT{i}", [S, 2, 2, 2, SP], F32R) for i in range(2)]
        ctx_a = sb("ctx_a", [P, 2, 2 * SP])
        ctx_f = sb("ctx_f", [P, 2, GB, SP])
        ctxT = pair_of("ctxT", [P, PAIRS, COLS])
        aT = sb("aT", [P, KD, GB, SP])
        logit_a = sb("logit_a", [S, GB, E])
        logit = sb("logit", [S, GB, E])
        above = sb("above", [S, GB, E, E])
        same = sb("same", [S, GB, E, E])
        rank = sb("rank", [S, GB, E])
        keep = sb("keep", [S, GB, E])
        top = sb("top", [S, GB])
        wsum = sb("wsum", [S, GB])
        wrec = sb("wrec", [S, GB])
        gate = sb("gate", [S, GB, E])
        wT = pair_of("wT", [E, GB, SP])
        th = sb("th", [P, COLS])
        act_f = sb("act_f", [P, FT, COLS])
        sT = pair_of("sT", [P, FT, COLS])
        y = xn
        select_f = act_f[0:E, :, 0:P]
        clsb = h_res[0:NTOK, 0, :]
        onehot_sb = h_mid[0:BUCKETS, 0, 0:NREL]
        table_sb = h_mid[0:BUCKETS, 1, 0:HEADS]

        psS, psT, psC, psD = pb("psS"), pb("psT"), pb("psC"), pb("psD")

        consts_loaded = sem("consts_loaded")
        masks_ready = sem("masks_ready")
        masks_made = sem("masks_made")
        piece_loaded = [sem(f"piece_loaded{i}") for i in range(2)]
        piece_hi = sem("piece_hi")
        piece_split = sem("piece_split")
        posb_ready = sem("posb_ready")
        gate_hi = sem("gate_hi")
        gate_split = sem("gate_split")
        select_ready = sem("select_ready")
        pads_zero = sem("pads_zero")
        bias_done = sem("bias_done")
        bias_ready = sem("bias_ready")
        dense_done = sem("dense_done")
        taken = [sem("even_bank_taken"), sem("odd_bank_taken")]
        side_a = sem("side_a")
        scores_done, scores_a, bias_added, scores_summed = map(sem, ("scores_done", "scores_a", "bias_added", "scores_summed"))
        max_ready, shifted, exp_done, sum_ready, recip_ready, probs_ready = map(
            sem, ("max_ready", "shifted", "exp_done", "sum_ready", "recip_ready", "probs_ready"))
        probsT_done, probsT_hi, probsT_lo = map(sem, ("probsT_done", "probsT_hi", "probsT_lo"))
        ctx_done, ctx_a_ready, ctx_summed, ctx_hi, ctx_lo = map(sem, ("ctx_done", "ctx_a_ready", "ctx_summed", "ctx_hi", "ctx_lo"))
        x_loaded, x_hi, x_split, txt_loaded, mid_loaded, res_loaded, stored = map(
            sem, ("x_loaded", "x_hi", "x_split", "txt_loaded", "mid_loaded", "res_loaded", "stored"))
        tok_scaled, tok_gamma, tok_final = map(sem, ("tok_scaled", "tok_gamma", "tok_final"))
        ln_aggr, ln_var, ln_rstd, ln_shift, ln_out = ({k: sem(f"{nm}_{k}") for k in ln} for nm in (
            "ln_aggr", "ln_var", "ln_rstd", "ln_shift", "ln_out"))
        top2_step, logit_exp, gate_ready = map(sem, ("top2_step", "logit_exp", "gate_ready"))
        tanh_ready, s_hi, s_lo = map(sem, ("tanh_ready", "s_hi", "s_lo"))

        def part(w, *index):
            return [t[(slice(None), *index)] for t in w]

        tok_pieces = [(wtok[:, 3 * i:3 * i + 3, :], *part(Wtok, slice(3 * i, 3 * i + 3))) for i in range(2)]
        qkv_pieces = [(wqkv[p], *part(Wqkv, p)) for p in range(PAIRS)]
        wo_pieces = [(wo[:, i:min(i + 3, PAIRS), :], *part(Wo, slice(i, min(i + 3, PAIRS)))) for i in (0, 3, 6)]
        up_pieces = [(wup[t], *part(Wup, t)) for t in range(FT)]
        down_pieces = [(wdown[:, i:i + 2, :], *part(Wdown, slice(i, i + 2))) for i in (0, 2)]
        pieces = tok_pieces + qkv_pieces[:4]
        for a, b in zip(wo_pieces, qkv_pieces[4:7]):
            pieces += [a, b]
        pieces += qkv_pieces[7:] + up_pieces + down_pieces
        qkv_index = [2, 3, 4, 5, 7, 9, 11, 12]
        FIRST = 3
        split_slot = {(-1, 2): 3, (-1, 6): 4, (-1, 9): 5, (-1, 11): 6}
        split_slot.update({(0, n): 7 + n for n in range(len(pieces) - 7)})

        def staged(i):
            shape = pieces[i][1].shape
            v = stage[:, i % 2, 0:int(np.prod(shape[1:]))]
            if len(shape) == 3:
                return v.rearrange("p (a b) -> p a b", a=shape[1])
            return v.rearrange("p (a b c) -> p a b c", a=shape[1], b=shape[2])

        def images(ap):
            return ap.rearrange("p (b s) -> p b s", b=GB)

        def rows(ap):
            return ap.rearrange("p (b e) -> p b e", b=2)

        block = ctx.enter_context(nc.Block())

        @block.sync
        def _(sp):
            def load_piece(i):
                if i >= 2:
                    sp.wait_ge(piece_split, i - 1)
                sp.dma_start(staged(i), pieces[i][0]).then_inc(piece_loaded[i % 2], 16)

            def group_of(t, first, count):
                return t[first:first + count] if isinstance(first, int) else t[bass.ds(first, count)]

            def body(g):
                y_jobs = [Job(g, "yback", h) if exists(g, -1) else None for h in range(2)]
                value = {name: v if isinstance(v, int) else sp.snap(v) for name, v in (
                    ("x", g + 1), ("txt", g * GB + GB), ("out0", g * GB - GB), ("out1", g * GB + (2 - GB)),
                    ("split", g + 1), ("moved", g * 16 + 16), ("group", g + 2), ("stored", g * 32),
                    *((f"y{h}", job.before + 1) for h, job in enumerate(y_jobs) if job))}
                if exists(g, 1) and not (isinstance(g, int) and g < 0):
                    sp.wait_ge(x_split, value["split"])
                    sp.dma_start(x_raw[:], group_of(xp, value["x"], 1).rearrange("o p k n -> p (o k) n")).then_inc(x_loaded, 16)
                if exists(g, 1):
                    at_least(sp, mid_loaded, value["moved"])
                    sp.dma_start(h_new[NTOK:S, :, :],
                                 group_of(txt, value["txt"], GB).rearrange("b t e -> t b e")).then_inc(txt_loaded, 16)
                for i in {-1: range(3, 6), 0: range(7, len(pieces))}.get(g, []) if isinstance(g, int) else []:
                    load_piece(i)
                for h, job in enumerate(y_jobs):
                    if job:
                        sp.wait_ge(taken[job.bank], value[f"y{h}"])
                        sp.dma_start(group_of(out, value[f"out{h}"], 2).rearrange("b s e -> s b e"),
                                     y[:, 2 * h:2 * h + 2, :]).then_inc(stored, 16)
                if exists(g, 0):
                    at_least(sp, stored, value["stored"])
                    sp.wait_ge(mid_loaded, value["moved"])
                    sp.dma_start(h_res[:], h_mid[:]).then_inc(res_loaded, 16)
                if exists(g, 1):
                    sp.wait_ge(ln_out["front"], value["group"])
                    at_least(sp, res_loaded, value["moved"])
                    sp.dma_start(h_mid[:], h_new[:]).then_inc(mid_loaded, 16)
                if isinstance(g, int) and g == -1:
                    load_piece(6)

            sp.dma_start(x_raw[:], xp[0:1].rearrange("o p k n -> p (o k) n")).then_inc(x_loaded, 16)
            load_piece(0)
            load_piece(1)
            for dst, src in ((onehot_sb, onehot), (table_sb, table), (posb[:], pos), (h_res[0:1, 0, :], cls),
                             (h_res[1:NTOK, 0, :], btok.partition_broadcast(NPATCH)),
                             (gammab[:], gamma.partition_broadcast(NTOK)),
                             (betab[:], beta.partition_broadcast(NTOK)), (gate_f[:], gatew)):
                sp.dma_start(dst, src).then_inc(consts_loaded, 16)
            load_piece(2)
            body(-1)
            body(0)
            with sp.Fori(LOOP_FROM, LOOP_TO) as g:
                body(g)
            body(GROUPS - 1)
            body(GROUPS)
            sp.wait_ge(stored, 16 * 2 * GROUPS)

        @block.tensor
        def _(pe):
            def three(out_ap, w, x, first, last):
                pe.matmul(out_ap, w[0], x[0], start=first, stop=False)
                pe.matmul(out_ap, w[0], x[1], start=False, stop=False)
                return pe.matmul(out_ap, w[1], x[0], start=False, stop=last)

            def wait_taken(*jobs):
                for job in jobs:
                    pe.wait_ge(taken[job.bank], job.before + 1)

            def dense(g, kind, i):
                job = Job(g, kind, i)
                ps = psD[:, job.bank, :]
                at_least(pe, taken[job.bank], job.before)
                if kind == "tok":
                    pe.wait_ge(x_split, g + 2)
                    for kt in range(KT):
                        pe.matmul(ps[:, 0:2 * PCOLS], Wtok[0][:, kt, P * i:P * i + P],
                                  x_pix[:, kt, :, :], start=(kt == 0), stop=False)
                        mm = pe.matmul(ps[:, PCOLS:2 * PCOLS], Wtok[1][:, kt, P * i:P * i + P],
                                       x_pix[:, kt, 0, :], start=False, stop=(kt == KT - 1))
                elif kind == "tback":
                    wait_taken(Job(g, "tok", 0), Job(g, "tok", 1))
                    for b in range(2):
                        for m in range(KD):
                            at = D * b + P * m
                            col = NTOK * (2 * i + b)
                            mm = pe.transpose(ps[0:S, at:at + P], tokT[:, m, col:col + S], ident[:, :])
                elif kind in ("xf", "xb"):
                    pe.wait_ge(ln_out["front" if kind == "xf" else "back"], g + 2 if kind == "xf" else g + 0)
                    for b in range(GB):
                        mm = pe.transpose(ps[:, SP * b:SP * b + S], xn[:, b, P * i:P * i + P], ident[0:S, 0:S])
                elif kind in ("q", "k", "vT"):
                    which = ("q", "k", "vT").index(kind)
                    if i == PAIRS and kind == "q":
                        wait_taken(Job(g, "xf", 0), Job(g, "xf", 1))
                    for k in range(KD):
                        mm = three(ps[:, 0:COLS], [w[:, i % PAIRS, which, k, :] for w in Wqkv],
                                   [x[:, k, :, :] for x in XT], k == 0, k == KD - 1)
                elif kind == "vback":
                    wait_taken(projected(g, "vT", i))
                    for b in range(GB):
                        mm = pe.transpose(ps[0:S, P * b:P * b + P], vT[:, b, 0:S], ident[:, :])
                elif kind == "wo":
                    pe.wait_ge(ctx_lo, g * PAIRS)
                    for p in range(PAIRS):
                        mm = three(ps[:, 0:COLS], [w[:, p, P * i:P * i + P] for w in Wo],
                                   [c[:, p, :] for c in ctxT], p == 0, p == PAIRS - 1)
                elif kind in ("aback", "yback"):
                    src = "wo" if kind == "aback" else "down"
                    wait_taken(Job(g, src, 0), Job(g, src, 1))
                    for b in range(2):
                        for m in range(KD):
                            at = D * b + P * m
                            mm = pe.transpose(ps[0:S, at:at + P], aT[:, m, 2 * i + b, 0:S], ident[:, :])
                elif kind == "logit":
                    wait_taken(Job(g, "xb", 0), Job(g, "xb", 1))
                    for b in range(GB):
                        at = 2 * E * b
                        for k in range(KD):
                            pe.matmul(ps[0:S, at:at + 2 * E], XB[0][:, k, b, 0:S], Wgate[:, k, :, :],
                                      start=(k == 0), stop=False)
                            mm = pe.matmul(ps[0:S, at + E:at + 2 * E], XB[1][:, k, b, 0:S], Wgate[:, k, 0, :],
                                           start=False, stop=(k == KD - 1))
                elif kind in ("u", "v"):
                    for k in range(KD):
                        mm = three(ps[:, 0:COLS], [w[:, i, int(kind == "v"), k, :] for w in Wup],
                                   [x[:, k, :, :] for x in XB], k == 0, k == KD - 1)
                elif kind == "wT":
                    pe.wait_ge(gate_ready, g + 0)
                    for b in range(GB):
                        mm = pe.transpose(ps[0:E, SP * b:SP * b + S], gate[:, b, :], ident[0:S, 0:S])
                elif kind == "mix":
                    wait_taken(Job(g, "wT", 0))
                    pe.matmul(ps[:, 0:COLS], select[:, i, :], wT[0][:, :, :], start=True, stop=False)
                    mm = pe.matmul(ps[:, 0:COLS], select[:, i, :], wT[1][:, :, :], start=False, stop=True)
                elif kind == "down":
                    pe.wait_ge(s_lo, g * FT)
                    for t in range(FT):
                        mm = three(ps[:, 0:COLS], [w[:, t, P * i:P * i + P] for w in Wdown],
                                   [x[:, t, :] for x in sT], t == 0, t == FT - 1)
                mm.then_inc(dense_done, 1)

            def scores(g, m):
                p = m // 2
                if m % 2 == 0:
                    wait_taken(projected(g, "q", p), projected(g, "k", p))
                at_least(pe, scores_summed, g * SLOTS + m)
                for b in range(2):
                    img, at = 2 * (m % 2) + b, 256 * b
                    for h in range(2):
                        r = slice(DH * h, DH * h + DH)
                        pe.matmul(psS[0:S, h, at:at + 2 * SP], Q[p % 2][0][r, img, 0:S], K[p % 2][r, img, :, :],
                                  start=True, stop=False)
                        mm = pe.matmul(psS[0:S, h, at + SP:at + 2 * SP], Q[p % 2][1][r, img, 0:S],
                                       K[p % 2][r, img, 0, :], start=False, stop=True)
                mm.then_inc(scores_done, 1)

            def probs_transposed(g, m):
                pe.wait_ge(probs_ready, g * SLOTS + (m + 1))
                at_least(pe, probsT_lo, g * SLOTS + (m - 1))
                for b in range(2):
                    for h in range(2):
                        at = SP * (2 * b + h)
                        mm = pe.transpose(psT[0:S, m % 2, at:at + S], prob[:, m % 4, 2 * h + b, :], ident[0:S, 0:S])
                mm.then_inc(probsT_done, 1)

            def context(g, m):
                p = m // 2
                if m % 2 == 0:
                    wait_taken(projected(g, "vback", p))
                pe.wait_ge(probsT_lo, g * SLOTS + (m + 1))
                at_least(pe, ctx_summed, g * SLOTS + m)
                for b in range(2):
                    img = 2 * (m % 2) + b
                    pe.matmul(psC[:, b, 0:4 * SP], V[p % 2][0][:, img, :], PT[m % 2][:, b, :, :, :],
                              start=True, stop=False)
                    mm = pe.matmul(psC[:, b, 2 * SP:4 * SP], V[p % 2][1][:, img, :], PT[m % 2][:, b, 0, :, :],
                                   start=False, stop=True)
                mm.then_inc(ctx_done, 1)

            def body(g):
                static = isinstance(g, int)
                for n in range(SLOTS):
                    fill, proj = slot_jobs(g, n)
                    if alive(g, n + 2):
                        scores(g, n + 2)
                    for kind, i in fill[:1]:
                        dense(g, kind, i)
                    if alive(g, n):
                        probs_transposed(g, n)
                    for kind, i in fill[1:]:
                        dense(g, kind, i)
                    if alive(g, n - 1):
                        context(g, n - 1)
                    for kind, i in proj:
                        if static and g < 1 and kind == "q" and PAIRS * g + i < PAIRS:
                            pe.wait_ge(piece_split, qkv_index[i % PAIRS] + 1)
                        dense(g, kind, i)

            pe.wait_ge(consts_loaded, 16 * 8)
            for k in range(S):
                at = HEADS * (k % 32)
                mm = pe.matmul((psS, psT, psC)[k // 32][0:S, 0, at:at + HEADS],
                               onehot_sb[:, S - 1 - k:2 * S - 1 - k], table_sb, start=True, stop=True)
            mm.then_inc(bias_done, 1)
            pe.wait_ge(masks_made, 3)
            pe.wait_ge(pads_zero, 1)
            pe.wait_ge(piece_split, 2)
            pe.wait_ge(bias_ready, 1)
            body(-1)
            body(0)
            pe.wait_ge(piece_split, len(pieces))
            pe.wait_ge(gate_split, 1)
            pe.wait_ge(select_ready, 1)
            with pe.Fori(LOOP_FROM, LOOP_TO) as g:
                body(g)
            body(GROUPS - 1)
            body(GROUPS)

        @block.scalar
        def _(act):
            def piece(i):
                act.wait_ge(piece_loaded[i % 2], 16 * (i // 2 + 1))
                act.copy(pieces[i][1], staged(i)).then_inc(piece_hi, 1)

            def dense(g, kind, i):
                if kind in ("tback", "aback", "yback", "v", "mix"):
                    return
                job = Job(g, kind, i)
                ps = psD[:, job.bank, :]
                act.wait_ge(dense_done, job.number + 1)
                if kind == "tok":
                    if i == 1:
                        last = Job(g, "tok", 0)
                        act.wait_ge(taken[last.bank], last.before + 1)
                    act.copy(tok_a[:], ps[:, 0:PCOLS]).then_inc(side_a, 1)
                elif kind in ("xf", "xb"):
                    act.copy((XT if kind == "xf" else XB)[0][:, i, :, 0:S],
                             images(ps[:, 0:COLS])[:, :, 0:S]).then_inc(side_a, 1)
                elif kind == "q":
                    at_least(act, scores_done, g * SLOTS + (2 * i - 2))
                    act.copy(Q[i % 2][0][:, :, :], images(ps[:, 0:COLS])).then_inc(side_a, 1)
                elif kind == "k":
                    act.copy(K[i % 2][:, :, 0, :], images(ps[:, 0:COLS])).then_inc(side_a, 1)
                elif kind == "vT":
                    act.copy(vT[:, :, :], images(ps[:, 0:COLS])).then_inc(taken[job.bank], 1)
                elif kind == "vback":
                    at_least(act, ctx_done, g * SLOTS + (2 * i - 2))
                    act.copy(V[i % 2][0][:, :, :], images(ps[0:S, :])).then_inc(side_a, 1)
                elif kind in ("wo", "down"):
                    act.copy(aT[:, i, :, :], images(ps[:, 0:COLS])).then_inc(taken[job.bank], 1)
                elif kind == "logit":
                    act.copy(logit_a[:], images(ps[0:S, 0:2 * E * GB])[:, :, 0:E]).then_inc(side_a, 1)
                elif kind == "u":
                    if i > 0:
                        last = Job(g, "u", i - 1)
                        act.wait_ge(taken[last.bank], last.before + 1)
                    act.activation(th[:], ps[:, 0:COLS], ACT.Tanh, scale=0.5).then_inc(tanh_ready, 1)
                elif kind == "wT":
                    act.copy(wT[0][:, :, 0:S], images(ps[0:E, 0:COLS])[:, :, 0:S]).then_inc(side_a, 1)

            def normalise(g, kind, off, src):
                act.wait_ge(ln_shift[kind], g + (off + 1))
                for b in range(GB):
                    last = act.activation(xn[:, b, :], src[:, b, :], ACT.Identity,
                                          bias=ln[kind]["nm"][:, b:b + 1], scale=ln[kind]["rs"][:, b:b + 1])
                last.then_inc(ln_out[kind], 1)

            def body(g):
                static = isinstance(g, int)
                for n in range(SLOTS):
                    fill, proj = slot_jobs(g, n)
                    if alive(g, n + 2):
                        m = n + 2
                        act.wait_ge(scores_done, g * SLOTS + (m + 1))
                        act.activation(prob[:, m % 4, :, :],
                                       psS[0:S, :, :].rearrange("p h (b c) -> p (h b) c", b=2)[:, :, 0:S],
                                       ACT.Copy, scale=SCALE).then_inc(scores_a, 1)
                    if alive(g, n + 1):
                        m = n + 1
                        act.wait_ge(shifted, g * SLOTS + (m + 1))
                        act.activation(prob[:, m % 4, :, :], prob[:, m % 4, :, :], ACT.Exp).then_inc(exp_done, 1)
                    for kind, i in fill[:1]:
                        dense(g, kind, i)
                    if alive(g, n):
                        m = n
                        act.wait_ge(probsT_done, g * SLOTS + (m + 1))
                        at_least(act, ctx_done, g * SLOTS + (m - 1))
                        act.copy(PT[m % 2][:, :, 0, :, 0:S],
                                 psT[0:S, m % 2, 0:4 * SP].rearrange("p (b h c) -> p b h c", b=2, h=2)[:, :, :, 0:S])\
                           .then_inc(probsT_hi, 1)
                    for kind, i in fill[1:]:
                        dense(g, kind, i)
                    if n == 9 and exists(g, -1):
                        act.wait_ge(top2_step, g * TOP2_STEPS + (5 - TOP2_STEPS))
                        act.activation(gate[:], gate[:], ACT.Exp).then_inc(logit_exp, 1)
                    if alive(g, n - 1):
                        m = n - 1
                        act.wait_ge(ctx_done, g * SLOTS + (m + 1))
                        at_least(act, ctx_summed, g * SLOTS + m)
                        act.copy(ctx_a[:, :, :], psC[:, :, 0:2 * SP]).then_inc(ctx_a_ready, 1)
                    for kind, i in proj:
                        dense(g, kind, i)
                    if n == 2 and exists(g, 1):
                        act.wait_ge(x_loaded, g * 16 + 32)
                        act.copy(x_pix[:, :, 0, :], x_raw[:, :, :]).then_inc(x_hi, 1)
                    if n == 5 and exists(g, -1):
                        normalise(g, "back", -1, h_res)
                    if n == 11 and exists(g, 1):
                        normalise(g, "front", 1, h_new)
                    if n == 11 and exists(g, -1):
                        for t in range(FT):
                            job = Job(g, "mix", t)
                            act.wait_ge(taken[job.bank], job.before + 1)
                            act.copy(sT[0][:, t, :], act_f[:, t, :]).then_inc(s_hi, 1)
                    if n % 2 == 0 and alive(g, n - 1):
                        m = n - 1
                        p = (m // 2) % PAIRS
                        act.wait_ge(ctx_summed, g * SLOTS + (m + 1))
                        act.copy(ctxT[0][:, p, :], ctx_f[:, p % 2, :, :].rearrange("p b s -> p (b s)")).then_inc(ctx_hi, 1)
                    if static and (g, n) in split_slot:
                        piece(split_slot[g, n])

            piece(0)
            piece(1)
            act.wait_ge(consts_loaded, 16 * 8)
            act.copy(Wgate[:, :, 0, :], gate_f[:, :, :]).then_inc(gate_hi, 1)
            act.wait_ge(masks_made, 3)
            act.copy(select[:], select_f).then_inc(select_ready, 1)
            act.wait_ge(pads_zero, 1)
            piece(2)
            body(-1)
            body(0)
            with act.Fori(LOOP_FROM, LOOP_TO) as g:
                body(g)
            body(GROUPS - 1)
            body(GROUPS)

        @block.vector
        def _(dve):
            def lo_part(lo, full, hi):
                return dve.tensor_tensor(lo, full, hi.bitcast(F32), ALU.subtract)

            def piece(i):
                dve.wait_ge(piece_hi, i + 1)
                lo_part(pieces[i][2], staged(i), pieces[i][1]).then_inc(piece_split, 1)

            def dense(g, kind, i):
                if kind in ("vT", "wo", "down"):
                    return
                job = Job(g, kind, i)
                ps = psD[:, job.bank, :]
                free = taken[job.bank]
                if kind in SIDED:
                    dve.wait_ge(side_a, job.sided)
                else:
                    dve.wait_ge(dense_done, job.number + 1)
                if kind == "tok":
                    dve.tensor_tensor(images(tokT[:, i, 0:GB * NTOK])[:, :, 1:NTOK], images(ps[:, PCOLS:2 * PCOLS]), images(tok_a[:]),
                                      ALU.add).then_inc(free, 1)
                elif kind == "tback":
                    at_least(dve, mid_loaded, g * 16 + 16)
                    dve.tensor_tensor(h_new[0:NTOK, 2 * i:2 * i + 2, :], rows(ps[0:NTOK, :]),
                                      posb[:].unsqueeze(1).to_broadcast((NTOK, 2, D)), ALU.add).then_inc(free, 1)
                elif kind in ("xf", "xb"):
                    X = XT if kind == "xf" else XB
                    lo_part(X[1][:, i, :, 0:S], images(ps[:, 0:COLS])[:, :, 0:S], X[0][:, i, :, 0:S]).then_inc(free, 1)
                elif kind == "q":
                    lo_part(Q[i % 2][1][:, :, :], images(ps[:, 0:COLS]), Q[i % 2][0][:, :, :]).then_inc(free, 1)
                elif kind == "k":
                    lo_part(K[i % 2][:, :, 1, :], images(ps[:, 0:COLS]), K[i % 2][:, :, 0, :]).then_inc(free, 1)
                elif kind == "vback":
                    lo_part(V[i % 2][1][:, :, :], images(ps[0:S, :]), V[i % 2][0][:, :, :]).then_inc(free, 1)
                elif kind == "aback":
                    dve.wait_ge(res_loaded, g * 16)
                    res = h_res[:, 2 * i:2 * i + 2, :]
                    dve.tensor_tensor(res, rows(ps[0:S, :]), res, ALU.add).then_inc(free, 1)
                elif kind == "yback":
                    dve.tensor_tensor(y[:, 2 * i:2 * i + 2, :], rows(ps[0:S, :]), h_res[:, 2 * i:2 * i + 2, :],
                                      ALU.add).then_inc(free, 1)
                elif kind == "logit":
                    dve.tensor_tensor(logit[:], images(ps[0:S, 0:2 * E * GB])[:, :, E:2 * E], logit_a[:],
                                      ALU.add).then_inc(free, 1)
                elif kind == "u":
                    dve.wait_ge(tanh_ready, g * FT + (i + 1 - FT))
                    dve.scalar_tensor_tensor(act_f[:, i, :], th[:], 1.0, ps[:, 0:COLS], ALU.add, ALU.mult).then_inc(free, 1)
                elif kind == "v":
                    before = Job(g, "u", i)
                    dve.wait_ge(taken[before.bank], before.before + 1)
                    dve.tensor_tensor(act_f[:, i, :], ps[:, 0:COLS], act_f[:, i, :], ALU.mult).then_inc(free, 1)
                elif kind == "wT":
                    lo_part(wT[1][:, :, 0:S], images(ps[0:E, 0:COLS])[:, :, 0:S], wT[0][:, :, 0:S]).then_inc(free, 1)
                elif kind == "mix":
                    dve.tensor_tensor(act_f[:, i, :], ps[:, 0:COLS], act_f[:, i, :], ALU.mult).then_inc(free, 1)

            def statistics(g, kind, off, src, n_rows):
                t = ln[kind]
                for b in range(GB):
                    dve.bn_stats(t["st"][0:n_rows, b, :], src[0:n_rows, b, :])
                dve.drain()
                for b in range(GB):
                    last = dve.bn_aggr(t["mv"][0:n_rows, b, :], t["st"][0:n_rows, b, :])
                last.then_inc(ln_aggr[kind], 1)
                dve.wait_ge(ln_aggr[kind], g + (off + 1))
                dve.tensor_scalar(t["ve"][0:n_rows, :], t["mv"][0:n_rows, :, 1], EPS, None, ALU.add).then_inc(ln_var[kind], 1)

            def shift_of(g, kind, off):
                t = ln[kind]
                dve.wait_ge(ln_rstd[kind], g + (off + 1))
                dve.scalar_tensor_tensor(t["nm"][:, :], t["mv"][:, :, 0], -1.0, t["rs"][:, :],
                                         ALU.mult, ALU.mult).then_inc(ln_shift[kind], 1)

            def top2(g, part_no):
                def step(k):
                    dve.wait_ge(top2_step, g * TOP2_STEPS + (k - TOP2_STEPS))

                four = (S, GB, E, E)
                if part_no == 0:
                    job = Job(g, "logit", 0)
                    dve.wait_ge(taken[job.bank], job.before + 1)
                    of_e = logit[:].unsqueeze(3).to_broadcast(four)
                    of_other = logit[:].unsqueeze(2).to_broadcast(four)
                    dve.tensor_tensor(above[:], of_other, of_e, ALU.is_gt).then_inc(top2_step, 1)
                    dve.tensor_tensor(same[:], of_other, of_e, ALU.is_equal).then_inc(top2_step, 1)
                    dve.tensor_reduce(top[:], logit[:], AX.X, ALU.max).then_inc(top2_step, 1)
                    step(2)
                    dve.tensor_tensor(same[:].rearrange("p b e f -> p b (e f)"), same[:].rearrange("p b e f -> p b (e f)"),
                                      earlier[0:S].rearrange("p e f -> p (e f)").unsqueeze(1).to_broadcast((S, GB, E * E)),
                                      ALU.mult).then_inc(top2_step, 1)
                    step(3)
                    dve.tensor_tensor(gate[:], logit[:], top[:].unsqueeze(2).to_broadcast((S, GB, E)),
                                      ALU.subtract).then_inc(top2_step, 1)
                    step(4)
                    dve.tensor_tensor(above[:], above[:], same[:], ALU.add).then_inc(top2_step, 1)
                    step(6)
                    dve.tensor_reduce(rank[:], above[:], AX.X, ALU.add).then_inc(top2_step, 1)
                    step(7)
                    dve.tensor_scalar(keep[:], rank[:], 1.5, None, ALU.is_lt).then_inc(top2_step, 1)
                else:
                    step(8)
                    dve.wait_ge(logit_exp, g + 0)
                    dve.tensor_tensor(gate[:], gate[:], keep[:], ALU.mult).then_inc(top2_step, 1)
                    step(9)
                    dve.tensor_reduce(wsum[:], gate[:], AX.X, ALU.add).then_inc(top2_step, 1)
                    step(10)
                    dve.reciprocal(wrec[:], wsum[:]).then_inc(top2_step, 1)
                    step(11)
                    dve.scalar_tensor_tensor(gate[:], gate[:], 0.5, wrec[:].unsqueeze(2).to_broadcast((S, GB, E)),
                                             ALU.mult, ALU.mult).then_inc(gate_ready, 1)

            def body(g):
                static = isinstance(g, int)
                for n in range(SLOTS):
                    fill, proj = slot_jobs(g, n)
                    for kind, i in fill[:1]:
                        dense(g, kind, i)
                    if alive(g, n + 1):
                        m = n + 1
                        dve.wait_ge(exp_done, g * SLOTS + (m + 1))
                        dve.tensor_reduce(sm[:, m % 2, :], prob[:, m % 4, :, :], AX.X, ALU.add).then_inc(sum_ready, 1)
                        dve.wait_ge(sum_ready, g * SLOTS + (m + 1))
                        dve.reciprocal(rc[:, m % 2, :], sm[:, m % 2, :]).then_inc(recip_ready, 1)
                    if alive(g, n + 2):
                        m = n + 2
                        dve.wait_ge(bias_added, g * SLOTS + (m + 1))
                        dve.scalar_tensor_tensor(
                            prob[:, m % 4, :, :],
                            psS[0:S, :, :].rearrange("p h (b c) -> p (h b) c", b=2)[:, :, SP:SP + S],
                            SCALE, prob[:, m % 4, :, :], ALU.mult, ALU.add).then_inc(scores_summed, 1)
                    if alive(g, n):
                        m = n
                        dve.wait_ge(probsT_hi, g * SLOTS + (m + 1))
                        lo_part(PT[m % 2][:, :, 1, :, 0:S],
                                psT[0:S, m % 2, 0:4 * SP].rearrange("p (b h c) -> p b h c", b=2, h=2)[:, :, :, 0:S],
                                PT[m % 2][:, :, 0, :, 0:S]).then_inc(probsT_lo, 1)
                    if alive(g, n + 2):
                        m = n + 2
                        dve.wait_ge(scores_summed, g * SLOTS + (m + 1))
                        dve.tensor_reduce(mx[:, m % 2, :], prob[:, m % 4, :, :], AX.X, ALU.max).then_inc(max_ready, 1)
                    for kind, i in fill[1:]:
                        dense(g, kind, i)
                    if n == 5 and exists(g, -1):
                        shift_of(g, "back", -1)
                    if n == 11 and exists(g, 1):
                        shift_of(g, "front", 1)
                    if alive(g, n - 1):
                        m = n - 1
                        p, img = (m // 2) % PAIRS, 2 * (m % 2)
                        dve.wait_ge(ctx_a_ready, g * SLOTS + (m + 1))
                        at_least(dve, ctx_lo, g * PAIRS + (m // 2 - 1))
                        for h in range(2):
                            r = slice(DH * h, DH * h + DH)
                            last = dve.tensor_tensor(ctx_f[r, p % 2, img:img + 2, :],
                                                     psC[r, :, SP * (2 + h):SP * (3 + h)],
                                                     ctx_a[r, :, SP * h:SP * h + SP], ALU.add)
                        last.then_inc(ctx_summed, 1)
                    for kind, i in proj:
                        dense(g, kind, i)
                    if exists(g, -1):
                        if n == 4:
                            last = Job(g, "aback", 1)
                            dve.wait_ge(taken[last.bank], last.before + 1)
                            statistics(g, "back", -1, h_res, S)
                        if n == 8:
                            top2(g, 0)
                        if n == 9:
                            top2(g, 1)
                    if exists(g, 1):
                        if n == 2:
                            dve.wait_ge(x_hi, g + 2)
                            lo_part(x_pix[:, :, 1, :], x_raw[:, :, :], x_pix[:, :, 0, :]).then_inc(x_split, 1)
                        if n == 6:
                            last = Job(g, "tback", 1)
                            dve.wait_ge(taken[last.bank], last.before + 1)
                            statistics(g, "tok", 1, h_new, NTOK)
                        if n == 7:
                            t = ln["tok"]
                            dve.wait_ge(ln_rstd["tok"], g + 2)
                            for b in range(GB):
                                last = dve.tensor_scalar(h_new[0:NTOK, b, :], h_new[0:NTOK, b, :], t["mv"][0:NTOK, b, 0:1],
                                                         t["rs"][0:NTOK, b:b + 1], ALU.subtract, ALU.mult)
                            last.then_inc(tok_scaled, 1)
                        if n == 10:
                            dve.wait_ge(tok_final, g * 2 + 4)
                            dve.wait_ge(txt_loaded, g * 16 + 32)
                            statistics(g, "front", 1, h_new, S)
                    if static and (g, n) in split_slot:
                        piece(split_slot[g, n])

            piece(0)
            piece(1)
            dve.wait_ge(consts_loaded, 16 * 8)
            dve.tensor_tensor(posb[:], posb[:], clsb, ALU.add).then_inc(posb_ready, 1)
            dve.wait_ge(gate_hi, 1)
            lo_part(Wgate[:, :, 1, :], gate_f[:, :, :], Wgate[:, :, 0, :]).then_inc(gate_split, 1)
            dve.wait_ge(bias_done, 1)
            for c in range(3):
                lo, hi = 32 * c, min(32 * c + 32, S)
                last = dve.tensor_copy(bias[:, :, lo:hi], (psS, psT, psC)[c][0:S, 0, 0:HEADS * (hi - lo)]
                                       .rearrange("p (k h) -> p h k", h=HEADS))
            last.then_inc(bias_ready, 1)
            dve.wait_ge(posb_ready, 1)
            dve.wait_ge(pads_zero, 1)
            dve.wait_ge(masks_made, 3)
            piece(2)
            body(-1)
            body(0)
            with dve.Fori(LOOP_FROM, LOOP_TO) as g:
                body(g)
            body(GROUPS - 1)
            body(GROUPS)

        @block.gpsimd
        def _(pool):
            def power(g, kind, off, n_rows):
                t = ln[kind]
                pool.wait_ge(ln_var[kind], g + (off + 1))
                pool.tensor_tensor(t["rs"][0:n_rows, :], t["ve"][0:n_rows, :], minus_half[0:n_rows, :],
                                   ALU.pow).then_inc(ln_rstd[kind], 1)

            def affine(g, i):
                half = h_new[0:NTOK, 2 * i:2 * i + 2, :]
                pool.tensor_tensor(half, half, gammab[:].unsqueeze(1).to_broadcast((NTOK, 2, D)), ALU.mult)\
                    .then_inc(tok_gamma, 1)
                pool.wait_ge(tok_gamma, g * 2 + (3 + i))
                pool.tensor_tensor(half, half, betab[:].unsqueeze(1).to_broadcast((NTOK, 2, D)), ALU.add)\
                    .then_inc(tok_final, 1)

            def body(g):
                for n in range(SLOTS):
                    if alive(g, n + 1):
                        m = n + 1
                        pool.wait_ge(max_ready, g * SLOTS + (m + 1))
                        pr = prob[:, m % 4, :, :]
                        pool.tensor_tensor(pr, pr, mx[:, m % 2, :].unsqueeze(2).to_broadcast((S, 4, S)),
                                           ALU.subtract).then_inc(shifted, 1)
                    if alive(g, n + 2):
                        m = n + 2
                        p = (m // 2) % PAIRS
                        pool.wait_ge(scores_a, g * SLOTS + (m + 1))
                        pr = prob[:, m % 4, :, :].rearrange("p (h b) k -> p h b k", h=2)
                        pool.tensor_tensor(pr, pr, bias[:, 2 * p:2 * p + 2, :].unsqueeze(2).to_broadcast((S, 2, 2, S)),
                                           ALU.add).then_inc(bias_added, 1)
                    if alive(g, n + 1):
                        m = n + 1
                        pool.wait_ge(recip_ready, g * SLOTS + (m + 1))
                        pr = prob[:, m % 4, :, :]
                        pool.tensor_tensor(pr, pr, rc[:, m % 2, :].unsqueeze(2).to_broadcast((S, 4, S)),
                                           ALU.mult).then_inc(probs_ready, 1)
                    if n % 2 == 0 and alive(g, n - 1):
                        m = n - 1
                        p = (m // 2) % PAIRS
                        pool.wait_ge(ctx_hi, g * PAIRS + (m // 2 + 1))
                        pool.tensor_tensor(ctxT[1][:, p, :], ctx_f[:, p % 2, :, :].rearrange("p b s -> p (b s)"),
                                           ctxT[0][:, p, :].bitcast(F32), ALU.subtract).then_inc(ctx_lo, 1)
                    if n == 4 and exists(g, -1):
                        power(g, "back", -1, S)
                    if n == 6 and exists(g, 1):
                        power(g, "tok", 1, NTOK)
                    if n in (8, 9) and exists(g, 1):
                        pool.wait_ge(tok_scaled, g + 2)
                        affine(g, n - 8)
                    if n == 10 and exists(g, 1):
                        power(g, "front", 1, S)
                    if n == 11 and exists(g, -1):
                        for t in range(FT):
                            pool.wait_ge(s_hi, g * FT + (t + 1 - FT))
                            pool.tensor_tensor(sT[1][:, t, :], act_f[:, t, :], sT[0][:, t, :].bitcast(F32),
                                               ALU.subtract).then_inc(s_lo, 1)

            pool.memset(ident[:], 0.0).then_inc(masks_ready, 1)
            pool.memset(select_f, 0.0).then_inc(masks_ready, 1)
            pool.memset(earlier[:], 1.0).then_inc(masks_ready, 1)
            pool.memset(minus_half[:], -0.5)
            for t in (*XT, *XB, *wT, *PT, tokT):
                last = pool.memset(t[:] if t is tokT else t[:].bitcast(F32), 0.0)
            last.then_inc(pads_zero, 1)
            pool.wait_ge(masks_ready, 3)
            pool.affine_select(out=ident[:], in_=ident[:], compare_op=ALU.not_equal, fill=1.0, base=0,
                               pattern=[[-1, P]], channel_multiplier=1).then_inc(masks_made, 1)
            sel = select_f.rearrange("e t (a r) -> e t a r", a=2)
            pool.affine_select(out=sel, in_=sel, compare_op=ALU.not_equal, fill=1.0, base=0,
                               pattern=[[-2, FT], [-1, 2], [0, R]], channel_multiplier=1).then_inc(masks_made, 1)
            pool.affine_select(out=earlier[:], in_=earlier[:], compare_op=ALU.is_gt, fill=0.0, base=0,
                               pattern=[[1, E], [-1, E]], channel_multiplier=0).then_inc(masks_made, 1)
            pool.wait_ge(bias_ready, 1)
            pool.wait_ge(consts_loaded, 16 * 8)
            body(-1)
            body(0)
            with pool.Fori(LOOP_FROM, LOOP_TO) as g:
                body(g)
            body(GROUPS - 1)
            body(GROUPS)


def bucket_one_hot():
    table = np.zeros((BUCKETS, NREL), np.float32)
    for i in range(NREL):
        rel = S - 1 - i
        dist = abs(rel)
        far = sum(dist >= edge for edge in (8, 12, 16, 23, 32, 46, 64))
        table[(dist if dist < 8 else 7 + far) + (16 if rel > 0 else 0), i] = 1.0
    return table


def kernel(**inputs):
    import concourse.bacc as bacc
    from concourse.bass_utils import run_bass_kernel_spmd

    a = {k: np.asarray(v) for k, v in inputs.items()}
    x = a["x"].reshape(GROUPS, GB, CHAN, SIDE, PATCH, SIDE, PATCH).transpose(0, 2, 4, 6, 1, 3, 5)
    x = x.reshape(GROUPS, KT, P, PCOLS).transpose(0, 2, 1, 3)
    qkv = np.stack([a["L0_attn_Wq"], a["L0_attn_Wk"], a["L0_attn_Wv"]]).reshape(3, KD, P, PAIRS, P)
    up = np.stack([a["L0_ffn_Wu"], a["L0_ffn_Wv"]]).reshape(2, FT, 2, KD, P, R)
    arrays = {
        "xp": x,
        "txt": a["txt"],
        "wtok": a["L0_tok_W"].reshape(KT, P, D).transpose(1, 0, 2),
        "btok": a["L0_tok_b"],
        "cls": a["L0_tok_cls_token"].reshape(1, D),
        "pos": a["L0_tok_pos_embedding"].reshape(NTOK, D),
        "gamma": a["L0_tok_gamma"],
        "beta": a["L0_tok_beta"],
        "wqkv": qkv.transpose(3, 2, 0, 1, 4),
        "wo": a["L0_attn_Wo"].reshape(PAIRS, P, D).transpose(1, 0, 2),
        "table": a["L0_attn_rel_bias_table"],
        "gatew": a["L0_ffn_gate_w"].reshape(KD, P, E).transpose(1, 0, 2),
        "wup": up.transpose(1, 4, 0, 3, 2, 5).reshape(FT, P, 2, KD, P),
        "wdown": a["L0_ffn_Wo"].reshape(FT, P, D).transpose(1, 0, 2),
        "onehot": bucket_one_hot(),
    }
    arrays = {k: np.ascontiguousarray(v) for k, v in arrays.items()}
    nc = bacc.Bacc("TRN2", target_bir_lowering=False, num_devices=1, dynamic_dma_scratch_size=1024)
    args = [nc.dram_tensor(k, v.shape, F32, kind="ExternalInput").ap() for k, v in arrays.items()]
    out = nc.dram_tensor("out", (BATCH, S, D), F32, kind="ExternalOutput").ap()
    build(nc, *args, out)
    r = run_bass_kernel_spmd(nc, [arrays], core_ids=[0])
    return r.results[0]["out"]
```

```python
from contextlib import ExitStack

import numpy as np

import concourse.bass as bass
from concourse import mybir

F32 = mybir.dt.float32
F32R = mybir.dt.float32r
ALU = mybir.AluOpType
ACT = mybir.ActivationFunctionType
AX = mybir.AxisListType

P = 128
BATCH, CHAN, IMG, PATCH = 32, 3, 96, 16
SIDE = IMG // PATCH
NPATCH = SIDE * SIDE
NTOK = NPATCH + 1
NTXT = 32
S = NTOK + NTXT
SP = S + 1
D = 256
KD = D // P
PDIM = CHAN * PATCH * PATCH
KT = PDIM // P
HEADS, DH = 16, 64
PAIRS = HEADS // 2
HALF = PAIRS // 2
GB = 4
GROUPS = BATCH // GB
COLS = GB * SP
PCOLS = GB * NPATCH
E, R = 8, 64
FT = E * R // P
SLOTS = 2 * PAIRS
NREL = 2 * S - 1
BUCKETS = 32
EPS = 1e-5
SCALE = DH ** -0.5
PIECE = 768
TOP2_STEPS = 11


def fillers(n):
    return {
        0: [("B", "woa", 1)],
        1: [("B", "wob", 0)],
        2: [("B", "wob", 1)],
        3: [("F", "tok", 0), ("B", "aback", 0), ("B", "aback", 1)],
        4: [("F", "tok", 1)],
        5: [("F", "tback", 0), ("F", "tback", 1)],
        6: [("B", "xb", 0), ("B", "xb", 1)],
        7: [("B", "logit", 0), ("B", "u", 0), ("B", "v", 0)],
        8: [("B", "u", 1), ("B", "v", 1)],
        9: [("B", "u", 2), ("B", "v", 2)],
        10: [("B", "u", 3), ("B", "v", 3), ("B", "wT", 0)],
        11: [("F", "xf", 0), ("F", "xf", 1), ("B", "mix", 0), ("B", "mix", 1)],
        12: [("A", "woa", 0), ("B", "mix", 2), ("B", "mix", 3)],
        13: [("B", "down", 0)],
        14: [("B", "down", 1)],
        15: [("B", "yback", 0), ("B", "yback", 1)],
    }.get(n, [])


def projections(n):
    if n % 2 == 1:
        return [("q", (n + 5) // 2), ("k", (n + 5) // 2)]
    return [("vback", (n + 2) // 2), ("vT", (n + 4) // 2)]


def exists(g, off):
    return not isinstance(g, int) or 0 <= g + off < GROUPS


def slot_jobs(g, n):
    off = {"F": 1, "A": 0, "B": -1}
    fill = [(k, i) for side, k, i in fillers(n) if exists(g, off[side])]
    proj = [(k, p) for k, p in projections(n) if exists(g, p // PAIRS)]
    return fill, proj


def body_jobs(g):
    return [j for n in range(SLOTS) for part in slot_jobs(g, n) for j in part]


SIDED = ("tok", "xf", "xb", "q", "k", "vback", "logit", "wT")
BANKS = 3
LOOP_FROM, LOOP_TO = 1, GROUPS - 1
BODY_LIST = {g: body_jobs(g) for g in range(-1, GROUPS + 1)}


def count_in(jobs, bank=None, sided=False):
    return sum((bank is None or at % BANKS == bank) and (not sided or kind in SIDED) for at, (kind, _) in enumerate(jobs))


class Job:

    def __init__(self, g, kind, i, off=0):
        static = isinstance(g, int)
        body = g + off if static else LOOP_FROM
        at = BODY_LIST[body].index((kind, i))
        self.bank = at % BANKS

        def total(upto, **which):
            before = sum(count_in(BODY_LIST[b], **which) for b in range(-1, body)) + count_in(BODY_LIST[body][:upto], **which)
            if static:
                return before
            per_body = count_in(BODY_LIST[LOOP_FROM], **which)
            return g * per_body + (before - per_body * (LOOP_FROM - off))

        self.number = total(at)
        self.before = total(at, bank=self.bank)
        self.sided = total(at + 1, sided=True)


def projected(g, kind, p):
    early = p < {"q": 3, "k": 3, "vT": 2, "vback": 1}[kind]
    return Job(g, kind, p + PAIRS, -1) if early else Job(g, kind, p)


def alive(g, m):
    return not isinstance(g, int) or 0 <= SLOTS * g + m < SLOTS * GROUPS


def at_least(eng, semaphore, value):
    if not isinstance(value, int) or value > 0:
        eng.wait_ge(semaphore, value)


def build(nc, xp, txt, wtok, btok, cls, pos, gamma, beta, wqkv, wo, table, gatew, wup, wdown, onehot, out):
    with ExitStack() as ctx:
        def sb(name, shape, dt=F32):
            return ctx.enter_context(nc.sbuf_tensor(name, shape, dt))

        def pb(name, banks):
            return ctx.enter_context(nc.psum_tensor(name, [P, banks, 512], F32))

        def sem(name):
            return ctx.enter_context(nc.semaphore(name))

        def pair_of(name, shape):
            return [sb(f"{name}_hi", shape, F32R), sb(f"{name}_lo", shape, F32R)]

        Wtok = pair_of("Wtok", [P, KT, D])
        Wqkv = pair_of("Wqkv", [P, PAIRS, 3, KD, P])
        Wo = pair_of("Wo", [P, PAIRS, D])
        Wup = pair_of("Wup", [P, FT, 2, KD, P])
        Wdown = pair_of("Wdown", [P, FT, D])
        Wgate = sb("Wgate", [P, KD, 2, E], F32R)
        stage = sb("stage", [P, 2, PIECE])
        ident = sb("ident", [P, P])
        select = sb("select", [E, FT, P], F32R)
        earlier = sb("earlier", [P, E, E])
        minus_half = sb("minus_half", [P, GB])
        posb = sb("posb", [NTOK, D])
        gammab = sb("gammab", [NTOK, D])
        betab = sb("betab", [NTOK, D])
        gate_f = sb("gate_f", [P, KD, E])
        bias = sb("bias", [S, HEADS, S])
        x_raw = sb("x_raw", [P, KT, PCOLS])
        x_pix = sb("x_pix", [P, KT, 2, PCOLS], F32R)
        tok_a = sb("tok_a", [P, PCOLS])
        tokT = sb("tokT", [P, KD, GB * NTOK + NTXT])
        h_new = sb("h_new", [S, GB, D])
        h_mid = sb("h_mid", [S, GB, D])
        h_res = sb("h_res", [S, GB, D])
        xn = sb("xn", [S, GB, D])
        XT = pair_of("XT", [P, KD, GB, SP])
        XB = pair_of("XB", [P, KD, GB, SP])
        ln = {k: dict(st=sb(f"st_{k}", [S, GB, 6]), mv=sb(f"mv_{k}", [S, GB, 2]), ve=sb(f"ve_{k}", [S, GB]),
                      rs=sb(f"rs_{k}", [S, GB]), nm=sb(f"nm_{k}", [S, GB])) for k in ("tok", "front", "back")}
        Q = [pair_of(f"Q{i}", [P, GB, SP]) for i in range(2)]
        K = [pair_of(f"K{i}", [P, GB, SP]) for i in range(2)]
        vT = sb("vT", [P, GB, SP])
        V = [pair_of(f"V{i}", [S, GB, P]) for i in range(2)]
        prob = sb("prob", [S, 4, 4, S])
        mx = sb("mx", [S, 4, 4])
        sm = sb("sm", [S, 4, 4])
        rc = sb("rc", [S, 4, 4])
        PT = [sb(f"PT{i}", [S, 2, 2, 2, SP], F32R) for i in range(2)]
        ctx_a = sb("ctx_a", [P, 2, 2 * SP])
        ctx_f = sb("ctx_f", [P, 2, GB, SP])
        ctxT = pair_of("ctxT", [P, PAIRS, COLS])
        aT = sb("aT", [P, KD, GB, SP])
        logit_a = sb("logit_a", [S, GB, E])
        logit = sb("logit", [S, GB, E])
        above = sb("above", [S, GB, E, E])
        same = sb("same", [S, GB, E, E])
        rank = sb("rank", [S, GB, E])
        keep = sb("keep", [S, GB, E])
        top = sb("top", [S, GB])
        wsum = sb("wsum", [S, GB])
        wrec = sb("wrec", [S, GB])
        gate = sb("gate", [S, GB, E])
        wT = pair_of("wT", [E, GB, SP])
        th = sb("th", [P, COLS])
        act_f = sb("act_f", [P, FT, COLS])
        sT = pair_of("sT", [P, FT, COLS])
        y = xn
        wo_part = stage[:].rearrange("p a b -> p (a b)")[:, 0:KD * COLS].rearrange("p (k n) -> p k n", k=KD)
        select_f = act_f[0:E, :, 0:P]
        clsb = h_res[0:NTOK, 0, :]
        onehot_sb = h_mid[0:BUCKETS, 0, 0:NREL]
        table_sb = h_mid[0:BUCKETS, 1, 0:HEADS]

        psS, psT, psC, psD = pb("psS", 2), pb("psT", 1), pb("psC", 2), pb("psD", BANKS)

        consts_loaded = sem("consts_loaded")
        masks_ready = sem("masks_ready")
        masks_made = sem("masks_made")
        piece_loaded = [sem(f"piece_loaded{i}") for i in range(2)]
        piece_hi = sem("piece_hi")
        piece_split = sem("piece_split")
        posb_ready = sem("posb_ready")
        gate_hi = sem("gate_hi")
        gate_split = sem("gate_split")
        select_ready = sem("select_ready")
        pads_zero = sem("pads_zero")
        bias_done = sem("bias_done")
        bias_ready = sem("bias_ready")
        dense_done = sem("dense_done")
        taken = [sem(f"bank{i}_taken") for i in range(BANKS)]
        side_a = sem("side_a")
        scores_done, scores_summed = map(sem, ("scores_done", "scores_summed"))
        max_ready, shifted, exp_done, sum_ready, recip_ready, probs_ready = map(
            sem, ("max_ready", "shifted", "exp_done", "sum_ready", "recip_ready", "probs_ready"))
        probsT_done, probsT_hi, probsT_lo = map(sem, ("probsT_done", "probsT_hi", "probsT_lo"))
        ctx_done, ctx_a_ready, ctx_summed, ctx_hi, ctx_lo = map(sem, ("ctx_done", "ctx_a_ready", "ctx_summed", "ctx_hi", "ctx_lo"))
        x_loaded, x_hi, x_split, txt_loaded, mid_loaded, res_loaded, stored = map(
            sem, ("x_loaded", "x_hi", "x_split", "txt_loaded", "mid_loaded", "res_loaded", "stored"))
        tok_gamma, tok_final = map(sem, ("tok_gamma", "tok_final"))
        ln_aggr, ln_var, ln_rstd, ln_shift, ln_out = ({k: sem(f"{nm}_{k}") for k in ln} for nm in (
            "ln_aggr", "ln_var", "ln_rstd", "ln_shift", "ln_out"))
        top2_step, logit_exp, gate_ready = map(sem, ("top2_step", "logit_exp", "gate_ready"))
        tanh_ready, s_hi, s_lo = map(sem, ("tanh_ready", "s_hi", "s_lo"))

        def part(w, *index):
            return [t[(slice(None), *index)] for t in w]

        tok_pieces = [(wtok[:, 3 * i:3 * i + 3, :], *part(Wtok, slice(3 * i, 3 * i + 3))) for i in range(2)]
        qkv_pieces = [(wqkv[p], *part(Wqkv, p)) for p in range(PAIRS)]
        wo_pieces = [(wo[:, i:min(i + 3, PAIRS), :], *part(Wo, slice(i, min(i + 3, PAIRS)))) for i in (0, 3, 6)]
        up_pieces = [(wup[t], *part(Wup, t)) for t in range(FT)]
        down_pieces = [(wdown[:, i:i + 2, :], *part(Wdown, slice(i, i + 2))) for i in (0, 2)]
        pieces = tok_pieces + qkv_pieces[:4]
        for a, b in zip(wo_pieces, qkv_pieces[4:7]):
            pieces += [a, b]
        pieces += qkv_pieces[7:] + up_pieces + down_pieces
        qkv_index = [2, 3, 4, 5, 7, 9, 11, 12]
        wo_index = 8
        FIRST = 3
        split_slot = {(-1, 2): 3, (-1, 6): 4, (-1, 9): 5, (-1, 11): 6}
        split_slot.update({(0, n): 7 + n for n in range(len(pieces) - 7)})

        def staged(i):
            shape = pieces[i][1].shape
            v = stage[:, i % 2, 0:int(np.prod(shape[1:]))]
            if len(shape) == 3:
                return v.rearrange("p (a b) -> p a b", a=shape[1])
            return v.rearrange("p (a b c) -> p a b c", a=shape[1], b=shape[2])

        def images(ap):
            return ap.rearrange("p (b s) -> p b s", b=GB)

        def rows(ap):
            return ap.rearrange("p (b e) -> p b e", b=2)

        block = ctx.enter_context(nc.Block())

        @block.sync
        def _(sp):
            def load_piece(i):
                if i >= 2:
                    sp.wait_ge(piece_split, i - 1)
                sp.dma_start(staged(i), pieces[i][0]).then_inc(piece_loaded[i % 2], 16)

            def group_of(t, first, count):
                return t[first:first + count] if isinstance(first, int) else t[bass.ds(first, count)]

            def moves(g):
                y_jobs = [Job(g, "yback", h, -1) if exists(g, -2) else None for h in range(2)]
                value = {name: v if isinstance(v, int) else sp.snap(v) for name, v in (
                    ("x", g + 1), ("txt", g * GB + GB), ("out0", g * GB - 2 * GB), ("out1", g * GB + (2 - 2 * GB)),
                    ("group", g + 1), ("loaded", g * 16), ("moved", g * 16 + 16), ("stored", g * 32 - 32),
                    *((f"y{h}", job.before + 1) for h, job in enumerate(y_jobs) if job))}
                early, late = {-1: (range(0), range(3, 7)), 0: (range(7, 9), range(9, len(pieces)))}.get(
                    g if isinstance(g, int) else None, (range(0), range(0)))
                if exists(g, 1) and not (isinstance(g, int) and g < 0):
                    sp.wait_ge(x_split, value["group"])
                    sp.dma_start(x_raw[:], group_of(xp, value["x"], 1).rearrange("o p k n -> p (o k) n")).then_inc(x_loaded, 16)
                for i in early:
                    load_piece(i)
                for h, job in enumerate(y_jobs):
                    if job:
                        sp.wait_ge(taken[job.bank], value[f"y{h}"])
                        sp.dma_start(group_of(out, value[f"out{h}"], 2).rearrange("b s e -> s b e"),
                                     y[:, 2 * h:2 * h + 2, :]).then_inc(stored, 16)
                if exists(g, -1):
                    at_least(sp, stored, value["stored"])
                    if isinstance(g, int):
                        sp.wait_ge(mid_loaded, value["loaded"])
                    sp.dma_start(h_res[:], h_mid[:]).then_inc(res_loaded, 16)
                if exists(g, 0):
                    at_least(sp, res_loaded, value["loaded"])
                    sp.wait_ge(ln_out["front"], value["group"])
                    sp.dma_start(h_mid[:], h_new[:]).then_inc(mid_loaded, 16)
                if exists(g, 1):
                    at_least(sp, mid_loaded, value["moved"])
                    sp.dma_start(h_new[NTOK:S, :, :],
                                 group_of(txt, value["txt"], GB).rearrange("b t e -> t b e")).then_inc(txt_loaded, 16)
                for i in late:
                    load_piece(i)

            sp.dma_start(x_raw[:], xp[0:1].rearrange("o p k n -> p (o k) n")).then_inc(x_loaded, 16)
            load_piece(0)
            load_piece(1)
            for dst, src in ((onehot_sb, onehot), (table_sb, table), (posb[:], pos), (h_res[0:1, 0, :], cls),
                             (h_res[1:NTOK, 0, :], btok.partition_broadcast(NPATCH)),
                             (gammab[:], gamma.partition_broadcast(NTOK)),
                             (betab[:], beta.partition_broadcast(NTOK)), (gate_f[:], gatew)):
                sp.dma_start(dst, src).then_inc(consts_loaded, 16)
            load_piece(2)
            for g in range(-1, LOOP_FROM + 1):
                moves(g)
            with sp.Fori(LOOP_FROM + 1, LOOP_TO) as g:
                moves(g)
            for g in range(LOOP_TO, GROUPS + 2):
                moves(g)
            sp.wait_ge(stored, 16 * 2 * GROUPS)

        @block.tensor
        def _(pe):
            def three(out_ap, w, x, first, last):
                pe.matmul(out_ap, w[0], x[0], start=first, stop=False)
                pe.matmul(out_ap, w[0], x[1], start=False, stop=False)
                return pe.matmul(out_ap, w[1], x[0], start=False, stop=last)

            def wait_taken(*jobs, before=None):
                for job in {job.bank: job for job in jobs if not before or job.bank != before.bank}.values():
                    pe.wait_ge(taken[job.bank], job.before + 1)

            def dense(g, kind, i):
                job = Job(g, kind, i)
                ps = psD[:, job.bank, :]
                at_least(pe, taken[job.bank], job.before)
                if kind == "tok":
                    pe.wait_ge(x_split, g + 2)
                    for kt in range(KT):
                        pe.matmul(ps[:, 0:2 * PCOLS], Wtok[0][:, kt, P * i:P * i + P],
                                  x_pix[:, kt, :, :], start=(kt == 0), stop=False)
                        mm = pe.matmul(ps[:, PCOLS:2 * PCOLS], Wtok[1][:, kt, P * i:P * i + P],
                                       x_pix[:, kt, 0, :], start=False, stop=(kt == KT - 1))
                elif kind == "tback":
                    wait_taken(Job(g, "tok", 0), Job(g, "tok", 1), before=job)
                    for b in range(2):
                        for m in range(KD):
                            at = D * b + P * m
                            col = NTOK * (2 * i + b)
                            mm = pe.transpose(ps[0:S, at:at + P], tokT[:, m, col:col + S], ident[:, :])
                elif kind in ("xf", "xb"):
                    pe.wait_ge(ln_out["front" if kind == "xf" else "back"], g + 2 if kind == "xf" else g + 0)
                    for b in range(GB):
                        mm = pe.transpose(ps[:, SP * b:SP * b + S], xn[:, b, P * i:P * i + P], ident[0:S, 0:S])
                elif kind in ("q", "k", "vT"):
                    which = ("q", "k", "vT").index(kind)
                    if i == PAIRS and kind == "q":
                        wait_taken(Job(g, "xf", 0), Job(g, "xf", 1), before=job)
                    for k in range(KD):
                        mm = three(ps[:, 0:COLS], [w[:, i % PAIRS, which, k, :] for w in Wqkv],
                                   [x[:, k, :, :] for x in XT], k == 0, k == KD - 1)
                elif kind == "vback":
                    wait_taken(projected(g, "vT", i), before=job)
                    for b in range(GB):
                        mm = pe.transpose(ps[0:S, P * b:P * b + P], vT[:, b, 0:S], ident[:, :])
                elif kind in ("woa", "wob"):
                    first = 0 if kind == "woa" else HALF
                    pe.wait_ge(ctx_lo, g * PAIRS + (HALF if (kind, i) == ("woa", 0) else first + HALF - PAIRS))
                    for p in range(first, first + HALF):
                        mm = three(ps[:, 0:COLS], [w[:, p, P * i:P * i + P] for w in Wo],
                                   [c[:, p, :] for c in ctxT], p == first, p == first + HALF - 1)
                elif kind in ("aback", "yback"):
                    src = "wob" if kind == "aback" else "down"
                    wait_taken(Job(g, src, 0), Job(g, src, 1), before=job)
                    for b in range(2):
                        for m in range(KD):
                            at = D * b + P * m
                            mm = pe.transpose(ps[0:S, at:at + P], aT[:, m, 2 * i + b, 0:S], ident[:, :])
                elif kind == "logit":
                    wait_taken(Job(g, "xb", 0), Job(g, "xb", 1), before=job)
                    for b in range(GB):
                        at = 2 * E * b
                        for k in range(KD):
                            pe.matmul(ps[0:S, at:at + 2 * E], XB[0][:, k, b, 0:S], Wgate[:, k, :, :],
                                      start=(k == 0), stop=False)
                            mm = pe.matmul(ps[0:S, at + E:at + 2 * E], XB[1][:, k, b, 0:S], Wgate[:, k, 0, :],
                                           start=False, stop=(k == KD - 1))
                elif kind in ("u", "v"):
                    for k in range(KD):
                        mm = three(ps[:, 0:COLS], [w[:, i, int(kind == "v"), k, :] for w in Wup],
                                   [x[:, k, :, :] for x in XB], k == 0, k == KD - 1)
                elif kind == "wT":
                    pe.wait_ge(gate_ready, g + 0)
                    for b in range(GB):
                        mm = pe.transpose(ps[0:E, SP * b:SP * b + S], gate[:, b, :], ident[0:S, 0:S])
                elif kind == "mix":
                    wait_taken(Job(g, "wT", 0), before=job)
                    pe.matmul(ps[:, 0:COLS], select[:, i, :], wT[0][:, :, :], start=True, stop=False)
                    mm = pe.matmul(ps[:, 0:COLS], select[:, i, :], wT[1][:, :, :], start=False, stop=True)
                elif kind == "down":
                    for t in range(FT):
                        if i == 0:
                            pe.wait_ge(s_lo, g * FT + (t + 1 - FT))
                        mm = three(ps[:, 0:COLS], [w[:, t, P * i:P * i + P] for w in Wdown],
                                   [x[:, t, :] for x in sT], t == 0, t == FT - 1)
                mm.then_inc(dense_done, 1)

            def scores(g, m):
                p = m // 2
                if m % 2 == 0:
                    wait_taken(projected(g, "q", p), projected(g, "k", p))
                at_least(pe, scores_summed, g * SLOTS + m)
                for b in range(2):
                    img = 2 * (m % 2) + b
                    for h in range(2):
                        r, at = slice(DH * h, DH * h + DH), SP * b
                        mm = three(psS[0:S, h, at:at + SP], [q[r, img, 0:S] for q in Q[p % 2]],
                                   [k[r, img, :] for k in K[p % 2]], True, True)
                mm.then_inc(scores_done, 1)

            def probs_transposed(g, m):
                pe.wait_ge(probs_ready, g * SLOTS + (m + 1))
                at_least(pe, probsT_lo, g * SLOTS + m)
                for b in range(2):
                    for h in range(2):
                        at = SP * (2 * b + h)
                        mm = pe.transpose(psT[0:S, 0, at:at + S], prob[:, m % 4, 2 * h + b, :], ident[0:S, 0:S])
                mm.then_inc(probsT_done, 1)

            def context(g, m):
                p = m // 2
                if m % 2 == 0:
                    wait_taken(projected(g, "vback", p))
                pe.wait_ge(probsT_lo, g * SLOTS + (m + 1))
                at_least(pe, ctx_summed, g * SLOTS + m)
                for b in range(2):
                    img = 2 * (m % 2) + b
                    pe.matmul(psC[:, b, 0:4 * SP], V[p % 2][0][:, img, :], PT[m % 2][:, b, :, :, :],
                              start=True, stop=False)
                    mm = pe.matmul(psC[:, b, 2 * SP:4 * SP], V[p % 2][1][:, img, :], PT[m % 2][:, b, 0, :, :],
                                   start=False, stop=True)
                mm.then_inc(ctx_done, 1)

            def body(g):
                static = isinstance(g, int)
                for n in range(SLOTS):
                    fill, proj = slot_jobs(g, n)
                    if alive(g, n + 3):
                        scores(g, n + 3)
                    for kind, i in fill[:1]:
                        if static and (g, kind) == (0, "woa"):
                            pe.wait_ge(piece_split, wo_index + 1)
                        dense(g, kind, i)
                    if alive(g, n):
                        probs_transposed(g, n)
                    for kind, i in fill[1:]:
                        dense(g, kind, i)
                    if alive(g, n - 1):
                        context(g, n - 1)
                    for kind, i in proj:
                        if static and g < 1 and kind == "q" and PAIRS * g + i < PAIRS:
                            pe.wait_ge(piece_split, qkv_index[i % PAIRS] + 1)
                        dense(g, kind, i)

            pe.wait_ge(consts_loaded, 16 * 8)
            for k in range(S):
                at = HEADS * (k % 32)
                mm = pe.matmul((psS, psT, psC)[k // 32][0:S, 0, at:at + HEADS],
                               onehot_sb[:, S - 1 - k:2 * S - 1 - k], table_sb, start=True, stop=True)
            mm.then_inc(bias_done, 1)
            pe.wait_ge(masks_made, 3)
            pe.wait_ge(pads_zero, 1)
            pe.wait_ge(piece_split, 2)
            pe.wait_ge(bias_ready, 1)
            body(-1)
            body(0)
            pe.wait_ge(piece_split, len(pieces))
            pe.wait_ge(gate_split, 1)
            pe.wait_ge(select_ready, 1)
            with pe.Fori(LOOP_FROM, LOOP_TO) as g:
                body(g)
            body(GROUPS - 1)
            body(GROUPS)

        @block.scalar
        def _(act):
            def piece(i):
                act.wait_ge(piece_loaded[i % 2], 16 * (i // 2 + 1))
                act.copy(pieces[i][1], staged(i)).then_inc(piece_hi, 1)

            def dense(g, kind, i):
                if kind in ("tback", "wob", "aback", "yback", "v", "mix"):
                    return
                job = Job(g, kind, i)
                ps = psD[:, job.bank, :]
                act.wait_ge(dense_done, job.number + 1)
                if kind == "tok":
                    if i == 1:
                        last = Job(g, "tok", 0)
                        act.wait_ge(taken[last.bank], last.before + 1)
                    act.copy(tok_a[:], ps[:, 0:PCOLS]).then_inc(side_a, 1)
                elif kind in ("xf", "xb"):
                    act.copy((XT if kind == "xf" else XB)[0][:, i, :, 0:S],
                             images(ps[:, 0:COLS])[:, :, 0:S]).then_inc(side_a, 1)
                elif kind == "q":
                    at_least(act, scores_done, g * SLOTS + (2 * i - 2))
                    act.copy(Q[i % 2][0][:, :, :], images(ps[:, 0:COLS])).then_inc(side_a, 1)
                elif kind == "k":
                    act.copy(K[i % 2][0][:, :, :], images(ps[:, 0:COLS])).then_inc(side_a, 1)
                elif kind == "vT":
                    act.copy(vT[:, :, :], images(ps[:, 0:COLS])).then_inc(taken[job.bank], 1)
                elif kind == "vback":
                    at_least(act, ctx_done, g * SLOTS + (2 * i - 2))
                    act.copy(V[i % 2][0][:, :, :], images(ps[0:S, :])).then_inc(side_a, 1)
                elif kind == "woa":
                    if isinstance(g, int) and g == 0 and i == 0:
                        act.wait_ge(piece_split, len(pieces))
                    act.copy(wo_part[:, i, :], ps[:, 0:COLS]).then_inc(taken[job.bank], 1)
                elif kind == "down":
                    act.copy(aT[:, i, :, :], images(ps[:, 0:COLS])).then_inc(taken[job.bank], 1)
                elif kind == "logit":
                    act.copy(logit_a[:], images(ps[0:S, 0:2 * E * GB])[:, :, 0:E]).then_inc(side_a, 1)
                elif kind == "u":
                    if i > 0:
                        last = Job(g, "u", i - 1)
                        act.wait_ge(taken[last.bank], last.before + 1)
                    act.activation(th[:], ps[:, 0:COLS], ACT.Tanh, scale=0.5).then_inc(tanh_ready, 1)
                elif kind == "wT":
                    act.copy(wT[0][:, :, 0:S], images(ps[0:E, 0:COLS])[:, :, 0:S]).then_inc(side_a, 1)

            def normalise(g, kind, off, src):
                act.wait_ge(ln_shift[kind], g + (off + 1))
                for b in range(GB):
                    last = act.activation(xn[:, b, :], src[:, b, :], ACT.Identity,
                                          bias=ln[kind]["nm"][:, b:b + 1], scale=ln[kind]["rs"][:, b:b + 1])
                last.then_inc(ln_out[kind], 1)

            def body(g):
                static = isinstance(g, int)
                for n in range(SLOTS):
                    fill, proj = slot_jobs(g, n)
                    if alive(g, n + 2):
                        m = n + 2
                        act.wait_ge(shifted, g * SLOTS + (m + 1))
                        act.activation(prob[:, m % 4, :, :], prob[:, m % 4, :, :], ACT.Exp, scale=SCALE).then_inc(exp_done, 1)
                    for kind, i in fill[:1]:
                        dense(g, kind, i)
                    if alive(g, n):
                        m = n
                        act.wait_ge(probsT_done, g * SLOTS + (m + 1))
                        at_least(act, ctx_done, g * SLOTS + (m - 1))
                        act.copy(PT[m % 2][:, :, 0, :, 0:S],
                                 psT[0:S, 0, 0:4 * SP].rearrange("p (b h c) -> p b h c", b=2, h=2)[:, :, :, 0:S])\
                           .then_inc(probsT_hi, 1)
                    for kind, i in fill[1:]:
                        dense(g, kind, i)
                    if n == 9 and exists(g, -1):
                        act.wait_ge(top2_step, g * TOP2_STEPS + (5 - TOP2_STEPS))
                        act.activation(gate[:], gate[:], ACT.Exp).then_inc(logit_exp, 1)
                    if alive(g, n - 1):
                        m = n - 1
                        act.wait_ge(ctx_done, g * SLOTS + (m + 1))
                        at_least(act, ctx_summed, g * SLOTS + m)
                        act.copy(ctx_a[:, :, :], psC[:, :, 0:2 * SP]).then_inc(ctx_a_ready, 1)
                    for kind, i in proj:
                        dense(g, kind, i)
                    if n == 0 and exists(g, 1):
                        act.wait_ge(x_loaded, g * 16 + 32)
                        act.copy(x_pix[:, :, 0, :], x_raw[:, :, :]).then_inc(x_hi, 1)
                    if n == 5 and exists(g, -1):
                        normalise(g, "back", -1, h_res)
                    if n == 10 and exists(g, 1):
                        normalise(g, "front", 1, h_new)
                    if n in (11, 12) and exists(g, -1):
                        for t in range(2 * (n - 11), 2 * (n - 10)):
                            job = Job(g, "mix", t)
                            act.wait_ge(taken[job.bank], job.before + 1)
                            act.copy(sT[0][:, t, :], act_f[:, t, :]).then_inc(s_hi, 1)
                    if n % 2 == 0 and alive(g, n - 1):
                        m = n - 1
                        p = (m // 2) % PAIRS
                        act.wait_ge(ctx_summed, g * SLOTS + (m + 1))
                        act.copy(ctxT[0][:, p, :], ctx_f[:, p % 2, :, :].rearrange("p b s -> p (b s)")).then_inc(ctx_hi, 1)
                    if static and (g, n) in split_slot:
                        piece(split_slot[g, n])

            piece(0)
            piece(1)
            act.wait_ge(consts_loaded, 16 * 8)
            act.copy(Wgate[:, :, 0, :], gate_f[:, :, :]).then_inc(gate_hi, 1)
            act.wait_ge(masks_made, 3)
            act.copy(select[:], select_f).then_inc(select_ready, 1)
            act.wait_ge(pads_zero, 1)
            piece(2)
            body(-1)
            body(0)
            with act.Fori(LOOP_FROM, LOOP_TO) as g:
                body(g)
            body(GROUPS - 1)
            body(GROUPS)

        @block.vector
        def _(dve):
            def lo_part(lo, full, hi):
                return dve.tensor_tensor(lo, full, hi.bitcast(F32), ALU.subtract)

            def piece(i):
                dve.wait_ge(piece_hi, i + 1)
                lo_part(pieces[i][2], staged(i), pieces[i][1]).then_inc(piece_split, 1)

            def dense(g, kind, i):
                if kind in ("vT", "woa", "down"):
                    return
                job = Job(g, kind, i)
                ps = psD[:, job.bank, :]
                free = taken[job.bank]
                if kind in SIDED:
                    dve.wait_ge(side_a, job.sided)
                else:
                    dve.wait_ge(dense_done, job.number + 1)
                if kind == "tok":
                    dve.tensor_tensor(images(tokT[:, i, 0:GB * NTOK])[:, :, 1:NTOK], images(ps[:, PCOLS:2 * PCOLS]), images(tok_a[:]),
                                      ALU.add).then_inc(free, 1)
                elif kind == "tback":
                    at_least(dve, mid_loaded, g * 16 + 16)
                    dve.tensor_tensor(h_new[0:NTOK, 2 * i:2 * i + 2, :], rows(ps[0:NTOK, :]),
                                      posb[:].unsqueeze(1).to_broadcast((NTOK, 2, D)), ALU.add).then_inc(free, 1)
                elif kind in ("xf", "xb"):
                    X = XT if kind == "xf" else XB
                    lo_part(X[1][:, i, :, 0:S], images(ps[:, 0:COLS])[:, :, 0:S], X[0][:, i, :, 0:S]).then_inc(free, 1)
                elif kind == "q":
                    lo_part(Q[i % 2][1][:, :, :], images(ps[:, 0:COLS]), Q[i % 2][0][:, :, :]).then_inc(free, 1)
                elif kind == "k":
                    lo_part(K[i % 2][1][:, :, :], images(ps[:, 0:COLS]), K[i % 2][0][:, :, :]).then_inc(free, 1)
                elif kind == "vback":
                    lo_part(V[i % 2][1][:, :, :], images(ps[0:S, :]), V[i % 2][0][:, :, :]).then_inc(free, 1)
                elif kind == "wob":
                    first = Job(g, "woa", 0, -1) if i == 0 else Job(g, "woa", 1)
                    dve.wait_ge(taken[first.bank], first.before + 1)
                    dve.tensor_tensor(aT[:, i, :, :], images(ps[:, 0:COLS]), images(wo_part[:, i, :]),
                                      ALU.add).then_inc(free, 1)
                elif kind == "aback":
                    dve.wait_ge(res_loaded, g * 16)
                    res = h_res[:, 2 * i:2 * i + 2, :]
                    dve.tensor_tensor(res, rows(ps[0:S, :]), res, ALU.add).then_inc(free, 1)
                elif kind == "yback":
                    dve.tensor_tensor(y[:, 2 * i:2 * i + 2, :], rows(ps[0:S, :]), h_res[:, 2 * i:2 * i + 2, :],
                                      ALU.add).then_inc(free, 1)
                elif kind == "logit":
                    dve.tensor_tensor(logit[:], images(ps[0:S, 0:2 * E * GB])[:, :, E:2 * E], logit_a[:],
                                      ALU.add).then_inc(free, 1)
                elif kind == "u":
                    dve.wait_ge(tanh_ready, g * FT + (i + 1 - FT))
                    dve.scalar_tensor_tensor(act_f[:, i, :], th[:], 1.0, ps[:, 0:COLS], ALU.add, ALU.mult).then_inc(free, 1)
                elif kind == "v":
                    before = Job(g, "u", i)
                    dve.wait_ge(taken[before.bank], before.before + 1)
                    dve.tensor_tensor(act_f[:, i, :], ps[:, 0:COLS], act_f[:, i, :], ALU.mult).then_inc(free, 1)
                elif kind == "wT":
                    lo_part(wT[1][:, :, 0:S], images(ps[0:E, 0:COLS])[:, :, 0:S], wT[0][:, :, 0:S]).then_inc(free, 1)
                elif kind == "mix":
                    dve.tensor_tensor(act_f[:, i, :], ps[:, 0:COLS], act_f[:, i, :], ALU.mult).then_inc(free, 1)

            def statistics(g, kind, off, src, n_rows):
                t = ln[kind]
                for b in range(GB):
                    dve.bn_stats(t["st"][0:n_rows, b, :], src[0:n_rows, b, :])
                dve.drain()
                for b in range(GB):
                    last = dve.bn_aggr(t["mv"][0:n_rows, b, :], t["st"][0:n_rows, b, :])
                last.then_inc(ln_aggr[kind], 1)
                dve.wait_ge(ln_aggr[kind], g + (off + 1))
                dve.tensor_scalar(t["ve"][0:n_rows, :], t["mv"][0:n_rows, :, 1], EPS, None, ALU.add).then_inc(ln_var[kind], 1)

            def shift_of(g, kind, off):
                t = ln[kind]
                dve.wait_ge(ln_rstd[kind], g + (off + 1))
                dve.scalar_tensor_tensor(t["nm"][:, :], t["mv"][:, :, 0], -1.0, t["rs"][:, :],
                                         ALU.mult, ALU.mult).then_inc(ln_shift[kind], 1)

            def top2(g, part_no):
                def step(k):
                    dve.wait_ge(top2_step, g * TOP2_STEPS + (k - TOP2_STEPS))

                four = (S, GB, E, E)
                if part_no == 0:
                    job = Job(g, "logit", 0)
                    dve.wait_ge(taken[job.bank], job.before + 1)
                    of_e = logit[:].unsqueeze(3).to_broadcast(four)
                    of_other = logit[:].unsqueeze(2).to_broadcast(four)
                    dve.tensor_tensor(above[:], of_other, of_e, ALU.is_gt).then_inc(top2_step, 1)
                    dve.tensor_tensor(same[:], of_other, of_e, ALU.is_equal).then_inc(top2_step, 1)
                    dve.tensor_reduce(top[:], logit[:], AX.X, ALU.max).then_inc(top2_step, 1)
                    step(2)
                    dve.tensor_tensor(same[:].rearrange("p b e f -> p b (e f)"), same[:].rearrange("p b e f -> p b (e f)"),
                                      earlier[0:S].rearrange("p e f -> p (e f)").unsqueeze(1).to_broadcast((S, GB, E * E)),
                                      ALU.mult).then_inc(top2_step, 1)
                    step(3)
                    dve.tensor_tensor(gate[:], logit[:], top[:].unsqueeze(2).to_broadcast((S, GB, E)),
                                      ALU.subtract).then_inc(top2_step, 1)
                    step(4)
                    dve.tensor_tensor(above[:], above[:], same[:], ALU.add).then_inc(top2_step, 1)
                    step(6)
                    dve.tensor_reduce(rank[:], above[:], AX.X, ALU.add).then_inc(top2_step, 1)
                    step(7)
                    dve.tensor_scalar(keep[:], rank[:], 1.5, None, ALU.is_lt).then_inc(top2_step, 1)
                else:
                    step(8)
                    dve.wait_ge(logit_exp, g + 0)
                    dve.tensor_tensor(gate[:], gate[:], keep[:], ALU.mult).then_inc(top2_step, 1)
                    step(9)
                    dve.tensor_reduce(wsum[:], gate[:], AX.X, ALU.add).then_inc(top2_step, 1)
                    step(10)
                    dve.reciprocal(wrec[:], wsum[:]).then_inc(top2_step, 1)
                    step(11)
                    dve.scalar_tensor_tensor(gate[:], gate[:], 0.5, wrec[:].unsqueeze(2).to_broadcast((S, GB, E)),
                                             ALU.mult, ALU.mult).then_inc(gate_ready, 1)

            def body(g):
                static = isinstance(g, int)
                for n in range(SLOTS):
                    fill, proj = slot_jobs(g, n)
                    if n == 5 and exists(g, -1):
                        shift_of(g, "back", -1)
                    if n == 10 and exists(g, 1):
                        shift_of(g, "front", 1)
                    if alive(g, n + 2):
                        m = n + 2
                        dve.wait_ge(exp_done, g * SLOTS + (m + 1))
                        dve.tensor_reduce(sm[:, m % 4, :], prob[:, m % 4, :, :], AX.X, ALU.add).then_inc(sum_ready, 1)
                    for kind, i in fill[:1]:
                        dense(g, kind, i)
                    if alive(g, n + 2):
                        m = n + 2
                        dve.wait_ge(sum_ready, g * SLOTS + (m + 1))
                        dve.reciprocal(rc[:, m % 4, :], sm[:, m % 4, :]).then_inc(recip_ready, 1)
                    if alive(g, n + 3):
                        m = n + 3
                        p = (m // 2) % PAIRS
                        dve.wait_ge(scores_done, g * SLOTS + (m + 1))
                        dve.tensor_tensor(
                            prob[:, m % 4, :, :].rearrange("p (h b) k -> p h b k", h=2),
                            psS[0:S, :, 0:2 * SP].rearrange("p h (b k) -> p h b k", b=2)[:, :, :, 0:S],
                            bias[:, 2 * p:2 * p + 2, :].unsqueeze(2).to_broadcast((S, 2, 2, S)),
                            ALU.add).then_inc(scores_summed, 1)
                    if alive(g, n):
                        m = n
                        dve.wait_ge(probsT_hi, g * SLOTS + (m + 1))
                        lo_part(PT[m % 2][:, :, 1, :, 0:S],
                                psT[0:S, 0, 0:4 * SP].rearrange("p (b h c) -> p b h c", b=2, h=2)[:, :, :, 0:S],
                                PT[m % 2][:, :, 0, :, 0:S]).then_inc(probsT_lo, 1)
                    if alive(g, n + 3):
                        m = n + 3
                        dve.wait_ge(scores_summed, g * SLOTS + (m + 1))
                        dve.tensor_reduce(mx[:, m % 4, :], prob[:, m % 4, :, :], AX.X, ALU.max).then_inc(max_ready, 1)
                    for kind, i in fill[1:]:
                        dense(g, kind, i)
                    if alive(g, n - 1):
                        m = n - 1
                        p, img = (m // 2) % PAIRS, 2 * (m % 2)
                        dve.wait_ge(ctx_a_ready, g * SLOTS + (m + 1))
                        at_least(dve, ctx_lo, g * PAIRS + (m // 2 - 1))
                        for h in range(2):
                            r = slice(DH * h, DH * h + DH)
                            last = dve.tensor_tensor(ctx_f[r, p % 2, img:img + 2, :],
                                                     psC[r, :, SP * (2 + h):SP * (3 + h)],
                                                     ctx_a[r, :, SP * h:SP * h + SP], ALU.add)
                        last.then_inc(ctx_summed, 1)
                    for kind, i in proj:
                        dense(g, kind, i)
                    if exists(g, -1):
                        if n == 3:
                            last = Job(g, "aback", 1)
                            dve.wait_ge(taken[last.bank], last.before + 1)
                            statistics(g, "back", -1, h_res, S)
                        if n == 8:
                            top2(g, 0)
                        if n == 9:
                            top2(g, 1)
                    if exists(g, 1):
                        if n == 5:
                            last = Job(g, "tback", 1)
                            dve.wait_ge(taken[last.bank], last.before + 1)
                            statistics(g, "tok", 1, h_new, NTOK)
                        if n == 6:
                            t = ln["tok"]
                            for b in range(GB):
                                last = dve.scalar_tensor_tensor(h_new[0:NTOK, b, :], h_new[0:NTOK, b, :],
                                                                t["mv"][0:NTOK, b, 0:1], gammab[:], ALU.subtract, ALU.mult)
                            last.then_inc(tok_gamma, 1)
                        if n == 7:
                            t = ln["tok"]
                            dve.wait_ge(ln_rstd["tok"], g + 2)
                            dve.wait_ge(tok_gamma, g + 2)
                            for b in range(GB):
                                last = dve.scalar_tensor_tensor(h_new[0:NTOK, b, :], h_new[0:NTOK, b, :],
                                                                t["rs"][0:NTOK, b:b + 1], betab[:], ALU.mult, ALU.add)
                            last.then_inc(tok_final, 1)
                        if n == 8:
                            dve.wait_ge(tok_final, g + 2)
                            dve.wait_ge(txt_loaded, g * 16 + 32)
                            statistics(g, "front", 1, h_new, S)
                    if static and (g, n) in split_slot:
                        piece(split_slot[g, n])

            piece(0)
            piece(1)
            dve.wait_ge(consts_loaded, 16 * 8)
            dve.tensor_tensor(posb[:], posb[:], clsb, ALU.add).then_inc(posb_ready, 1)
            dve.wait_ge(gate_hi, 1)
            lo_part(Wgate[:, :, 1, :], gate_f[:, :, :], Wgate[:, :, 0, :]).then_inc(gate_split, 1)
            dve.wait_ge(bias_done, 1)
            for c in range(3):
                lo, hi = 32 * c, min(32 * c + 32, S)
                last = dve.tensor_scalar(bias[:, :, lo:hi], (psS, psT, psC)[c][0:S, 0, 0:HEADS * (hi - lo)]
                                         .rearrange("p (k h) -> p h k", h=HEADS), 1 / SCALE, None, ALU.mult)
            last.then_inc(bias_ready, 1)
            dve.wait_ge(posb_ready, 1)
            dve.wait_ge(pads_zero, 1)
            dve.wait_ge(masks_made, 3)
            piece(2)
            body(-1)
            body(0)
            with dve.Fori(LOOP_FROM, LOOP_TO) as g:
                body(g)
            body(GROUPS - 1)
            body(GROUPS)

        @block.gpsimd
        def _(pool):
            def power(g, kind, off, n_rows):
                t = ln[kind]
                pool.wait_ge(ln_var[kind], g + (off + 1))
                pool.tensor_tensor(t["rs"][0:n_rows, :], t["ve"][0:n_rows, :], minus_half[0:n_rows, :],
                                   ALU.pow).then_inc(ln_rstd[kind], 1)

            def body(g):
                for n in range(SLOTS):
                    if alive(g, n + 2):
                        m = n + 2
                        pool.wait_ge(max_ready, g * SLOTS + (m + 1))
                        pr = prob[:, m % 4, :, :]
                        pool.tensor_tensor(pr, pr, mx[:, m % 4, :].unsqueeze(2).to_broadcast((S, 4, S)),
                                           ALU.subtract).then_inc(shifted, 1)
                    if alive(g, n + 1):
                        m = n + 1
                        pool.wait_ge(recip_ready, g * SLOTS + (m + 1))
                        pr = prob[:, m % 4, :, :]
                        pool.tensor_tensor(pr, pr, rc[:, m % 4, :].unsqueeze(2).to_broadcast((S, 4, S)),
                                           ALU.mult).then_inc(probs_ready, 1)
                    if n % 2 == 0 and alive(g, n - 1):
                        m = n - 1
                        p = (m // 2) % PAIRS
                        pool.wait_ge(ctx_hi, g * PAIRS + (m // 2 + 1))
                        pool.tensor_tensor(ctxT[1][:, p, :], ctx_f[:, p % 2, :, :].rearrange("p b s -> p (b s)"),
                                           ctxT[0][:, p, :].bitcast(F32), ALU.subtract).then_inc(ctx_lo, 1)
                    if n == 1 and exists(g, 1):
                        pool.wait_ge(x_hi, g + 2)
                        pool.tensor_tensor(x_pix[:, :, 1, :], x_raw[:, :, :], x_pix[:, :, 0, :].bitcast(F32),
                                           ALU.subtract).then_inc(x_split, 1)
                    if n == 4 and exists(g, -1):
                        power(g, "back", -1, S)
                    if n == 6 and exists(g, 1):
                        power(g, "tok", 1, NTOK)
                    if n == 9 and exists(g, 1):
                        power(g, "front", 1, S)
                    if n in (11, 12) and exists(g, -1):
                        for t in range(2 * (n - 11), 2 * (n - 10)):
                            pool.wait_ge(s_hi, g * FT + (t + 1 - FT))
                            pool.tensor_tensor(sT[1][:, t, :], act_f[:, t, :], sT[0][:, t, :].bitcast(F32),
                                               ALU.subtract).then_inc(s_lo, 1)

            pool.memset(ident[:], 0.0).then_inc(masks_ready, 1)
            pool.memset(select_f, 0.0).then_inc(masks_ready, 1)
            pool.memset(earlier[:], 1.0).then_inc(masks_ready, 1)
            pool.memset(minus_half[:], -0.5)
            for t in (*XT, *XB, *wT, *PT, tokT):
                last = pool.memset(t[:] if t is tokT else t[:].bitcast(F32), 0.0)
            last.then_inc(pads_zero, 1)
            pool.wait_ge(masks_ready, 3)
            pool.affine_select(out=ident[:], in_=ident[:], compare_op=ALU.not_equal, fill=1.0, base=0,
                               pattern=[[-1, P]], channel_multiplier=1).then_inc(masks_made, 1)
            sel = select_f.rearrange("e t (a r) -> e t a r", a=2)
            pool.affine_select(out=sel, in_=sel, compare_op=ALU.not_equal, fill=1.0, base=0,
                               pattern=[[-2, FT], [-1, 2], [0, R]], channel_multiplier=1).then_inc(masks_made, 1)
            pool.affine_select(out=earlier[:], in_=earlier[:], compare_op=ALU.is_gt, fill=0.0, base=0,
                               pattern=[[1, E], [-1, E]], channel_multiplier=0).then_inc(masks_made, 1)
            pool.wait_ge(bias_ready, 1)
            pool.wait_ge(consts_loaded, 16 * 8)
            body(-1)
            body(0)
            with pool.Fori(LOOP_FROM, LOOP_TO) as g:
                body(g)
            body(GROUPS - 1)
            body(GROUPS)


def bucket_one_hot():
    table = np.zeros((BUCKETS, NREL), np.float32)
    for i in range(NREL):
        rel = S - 1 - i
        dist = abs(rel)
        far = sum(dist >= edge for edge in (8, 12, 16, 23, 32, 46, 64))
        table[(dist if dist < 8 else 7 + far) + (16 if rel > 0 else 0), i] = 1.0
    return table


def kernel(**inputs):
    import concourse.bacc as bacc
    from concourse.bass_utils import run_bass_kernel_spmd

    a = {k: np.asarray(v) for k, v in inputs.items()}
    x = a["x"].reshape(GROUPS, GB, CHAN, SIDE, PATCH, SIDE, PATCH).transpose(0, 2, 4, 6, 1, 3, 5)
    x = x.reshape(GROUPS, KT, P, PCOLS).transpose(0, 2, 1, 3)
    qkv = np.stack([a["L0_attn_Wq"], a["L0_attn_Wk"], a["L0_attn_Wv"]]).reshape(3, KD, P, PAIRS, P)
    up = np.stack([a["L0_ffn_Wu"], a["L0_ffn_Wv"]]).reshape(2, FT, 2, KD, P, R)
    arrays = {
        "xp": x,
        "txt": a["txt"],
        "wtok": a["L0_tok_W"].reshape(KT, P, D).transpose(1, 0, 2),
        "btok": a["L0_tok_b"],
        "cls": a["L0_tok_cls_token"].reshape(1, D),
        "pos": a["L0_tok_pos_embedding"].reshape(NTOK, D),
        "gamma": a["L0_tok_gamma"],
        "beta": a["L0_tok_beta"],
        "wqkv": qkv.transpose(3, 2, 0, 1, 4),
        "wo": a["L0_attn_Wo"].reshape(PAIRS, P, D).transpose(1, 0, 2),
        "table": a["L0_attn_rel_bias_table"],
        "gatew": a["L0_ffn_gate_w"].reshape(KD, P, E).transpose(1, 0, 2),
        "wup": up.transpose(1, 4, 0, 3, 2, 5).reshape(FT, P, 2, KD, P),
        "wdown": a["L0_ffn_Wo"].reshape(FT, P, D).transpose(1, 0, 2),
        "onehot": bucket_one_hot(),
    }
    arrays = {k: np.ascontiguousarray(v) for k, v in arrays.items()}
    nc = bacc.Bacc("TRN2", target_bir_lowering=False, num_devices=1, dynamic_dma_scratch_size=1024)
    args = [nc.dram_tensor(k, v.shape, F32, kind="ExternalInput").ap() for k, v in arrays.items()]
    out = nc.dram_tensor("out", (BATCH, S, D), F32, kind="ExternalOutput").ap()
    build(nc, *args, out)
    r = run_bass_kernel_spmd(nc, [arrays], core_ids=[0])
    return r.results[0]["out"]
```

```python
from contextlib import ExitStack

import numpy as np

import concourse.bass as bass
from concourse import mybir

F32 = mybir.dt.float32
F32R = mybir.dt.float32r
ALU = mybir.AluOpType
ACT = mybir.ActivationFunctionType
AX = mybir.AxisListType

P = 128
BATCH, CHAN, IMG, PATCH = 32, 3, 96, 16
SIDE = IMG // PATCH
NPATCH = SIDE * SIDE
NTOK = NPATCH + 1
NTXT = 32
S = NTOK + NTXT
SP = S + 1
D = 256
KD = D // P
PDIM = CHAN * PATCH * PATCH
KT = PDIM // P
HEADS, DH = 16, 64
PAIRS = HEADS // 2
HALF = PAIRS // 2
GB = 4
GROUPS = BATCH // GB
COLS = GB * SP
PCOLS = GB * NPATCH
E, R = 8, 64
FT = E * R // P
SLOTS = 2 * PAIRS
NREL = 2 * S - 1
BUCKETS = 32
EPS = 1e-5
SCALE = DH ** -0.5
PIECE = 768
TOP2_STEPS = 11
TOP2_EXP = 11
FIRST_KEYS = 14


def fillers(n):
    return {
        1: [("B", "wob", 0), ("B", "wob", 1)],
        2: [("B", "aback", 0), ("B", "aback", 1)],
        3: [("F", "tok", 0)],
        4: [("F", "tok", 1)],
        5: [("F", "tback", 0), ("F", "tback", 1), ("B", "xb", 0), ("B", "xb", 1)],
        6: [("B", "logit", 0), ("B", "u", 0), ("B", "v", 0)],
        7: [("B", "u", 1), ("B", "v", 1)],
        8: [("B", "u", 2), ("B", "v", 2)],
        9: [("B", "u", 3)],
        10: [("B", "v", 3), ("A", "woa", 0)],
        11: [("F", "xf", 0), ("F", "xf", 1), ("A", "woa", 1)],
        12: [("B", "wT", 0), ("B", "mix", 0), ("B", "mix", 1), ("B", "mix", 2), ("B", "mix", 3)],
        13: [("B", "down", 0)],
        14: [("B", "down", 1)],
        15: [("B", "yback", 0), ("B", "yback", 1)],
    }.get(n, [])


def projections(n):
    if n % 2 == 1:
        return [("q", (n + 5) // 2), ("k", (n + 5) // 2)]
    return [("vback", (n + 2) // 2), ("vT", (n + 4) // 2)]


def parted(n, fill):
    a, b, c = {1: (0, 2, 2), 3: (0, 1, 1), 11: (2, 2, 3), 10: (1, 1, 2), 12: (0, 0, 1), 13: (0, 0, 0), 14: (0, 0, 0)}.get(n, (1, len(fill), len(fill)))
    return fill[:a], fill[a:b], fill[b:c], fill[c:]


def exists(g, off):
    return not isinstance(g, int) or 0 <= g + off < GROUPS


def last_body(g):
    return isinstance(g, int) and g == GROUPS


def slot_jobs(g, n):
    off = {"F": 1, "A": 0, "B": -1}
    fill = [job for job in fillers(n) if not (last_body(g) and job[1] == "wT")]
    if last_body(g) and n == 9:
        fill = fill + [("B", "wT", 0)]
    fill = parted(n, fill)
    fill = [[(k, i) for side, k, i in part if exists(g, off[side])] for part in fill]
    proj = [(k, p) for k, p in projections(n) if exists(g, p // PAIRS)]
    return *fill[:3], proj, fill[3]


def body_jobs(g):
    return [j for n in range(SLOTS) for part in slot_jobs(g, n) for j in part]


SIDED = ("tok", "xf", "xb", "logit", "wT")
BANKS = 3
LOOP_FROM, LOOP_TO = 1, GROUPS - 1
BODY_LIST = {g: body_jobs(g) for g in range(-1, GROUPS + 1)}


def bank_of(jobs, at):
    return 1 if at == len(jobs) - 1 and at % BANKS == 0 else at % BANKS


def count_in(jobs, upto=None, bank=None, sided=False):
    return sum((bank is None or bank_of(jobs, at) == bank) and (not sided or kind in SIDED)
               for at, (kind, _) in enumerate(jobs[:upto]))


class Job:

    def __init__(self, g, kind, i, off=0):
        static = isinstance(g, int)
        body = g + off if static else LOOP_FROM
        at = BODY_LIST[body].index((kind, i))
        self.bank = bank_of(BODY_LIST[body], at)

        def total(upto, **which):
            before = sum(count_in(BODY_LIST[b], **which) for b in range(-1, body)) + count_in(BODY_LIST[body], upto, **which)
            if static:
                return before
            per_body = count_in(BODY_LIST[LOOP_FROM], **which)
            return g * per_body + (before - per_body * (LOOP_FROM - off))

        self.number = total(at)
        self.before = total(at, bank=self.bank)
        self.sided = total(at + 1, sided=True)


def projected(g, kind, p):
    early = p < {"q": 3, "k": 3, "vT": 2, "vback": 1}[kind]
    return Job(g, kind, p + PAIRS, -1) if early else Job(g, kind, p)


def alive(g, m):
    return not isinstance(g, int) or 0 <= SLOTS * g + m < SLOTS * GROUPS


def at_least(eng, semaphore, value):
    if not isinstance(value, int) or value > 0:
        eng.wait_ge(semaphore, value)


def build(nc, xp, txt, wtok, btok, cls, pos, gamma, beta, wqkv, wo, table, gatew, wup, wdown, onehot, out):
    with ExitStack() as ctx:
        def sb(name, shape, dt=F32):
            return ctx.enter_context(nc.sbuf_tensor(name, shape, dt))

        def pb(name, banks):
            return ctx.enter_context(nc.psum_tensor(name, [P, banks, 512], F32))

        def sem(name):
            return ctx.enter_context(nc.semaphore(name))

        def pair_of(name, shape):
            return [sb(f"{name}_hi", shape, F32R), sb(f"{name}_lo", shape, F32R)]

        Wtok = pair_of("Wtok", [P, KT, D])
        Wqkv = pair_of("Wqkv", [P, PAIRS, 3, KD, P])
        Wo = pair_of("Wo", [P, PAIRS, D])
        Wup = pair_of("Wup", [P, FT, 2, KD, P])
        Wdown = pair_of("Wdown", [P, FT, D])
        Wgate = sb("Wgate", [P, KD, 2, E], F32R)
        stage = sb("stage", [P, 2, PIECE])
        ident = sb("ident", [P, P])
        select = sb("select", [E, FT, P], F32R)
        earlier = sb("earlier", [P, E, E])
        minus_half = sb("minus_half", [P, GB])
        posb = sb("posb", [NTOK, D])
        gammab = sb("gammab", [NTOK, D])
        betab = sb("betab", [NTOK, D])
        gate_f = sb("gate_f", [P, KD, E])
        bias = sb("bias", [S, HEADS, S])
        x_raw = sb("x_raw", [P, KT, PCOLS])
        x_pix = sb("x_pix", [P, KT, 2, PCOLS], F32R)
        tokT = sb("tokT", [P, KD, GB * NTOK + NTXT])
        h_new = sb("h_new", [S, GB, D])
        h_mid = sb("h_mid", [S, GB, D])
        h_res = sb("h_res", [S, GB, D])
        xn = sb("xn", [S, GB, D])
        XT = pair_of("XT", [P, KD, GB, SP])
        XB = pair_of("XB", [P, KD, GB, SP])
        ln = {k: dict(st=sb(f"st_{k}", [S, GB, 6]), mv=sb(f"mv_{k}", [S, GB, 2]), ve=sb(f"ve_{k}", [S, GB]),
                      rs=sb(f"rs_{k}", [S, GB]), nm=sb(f"nm_{k}", [S, GB])) for k in ("tok", "front", "back")}
        Q = [pair_of(f"Q{i}", [P, GB, SP]) for i in range(2)]
        K = [pair_of(f"K{i}", [P, GB, SP]) for i in range(2)]
        q_full = sb("q_full", [P, GB, SP])
        k_full = sb("k_full", [P, GB, SP])
        vT = sb("vT", [P, GB, SP])
        v_full = sb("v_full", [S, GB, P])
        V = [pair_of(f"V{i}", [S, GB, P]) for i in range(2)]
        prob = sb("prob", [S, 4, 4, S])
        mx = sb("mx", [S, 4, 4])
        sm = sb("sm", [S, 4, 4])
        rc = sb("rc", [S, 4, 4])
        PT = [sb(f"PT{i}", [S, 2, 2, 2, SP], F32R) for i in range(2)]
        ctx_a = sb("ctx_a", [P, 2, 2 * SP])
        ctx_f = sb("ctx_f", [P, 2, GB, SP])
        ctxT = pair_of("ctxT", [P, PAIRS, COLS])
        aT = sb("aT", [P, KD, GB, SP])
        top = sb("top", [S, GB])
        wsum = sb("wsum", [S, GB])
        wrec = sb("wrec", [S, GB])
        gate = sb("gate", [S, GB, E])
        wT = pair_of("wT", [E, GB, SP])
        act_f = sb("act_f", [P, FT, COLS])
        sT = pair_of("sT", [P, FT, COLS])
        ffn_v = aT[:].rearrange("p k b s -> p k (b s)")
        y = xn
        staging = stage[:].rearrange("p a b -> p (a b)")
        at = KD * COLS
        wo_part = staging[:, 0:at].rearrange("p (k n) -> p k n", k=KD)
        th = staging[:, at:at + COLS]
        at += COLS
        above, same = (staging[0:S, i:i + GB * E * E].rearrange("p (b e f) -> p b e f", b=GB, e=E)
                       for i in (at, at + GB * E * E))
        at += 2 * GB * E * E
        logit_a, logit, rank, keep = (staging[0:S, i:i + GB * E].rearrange("p (b e) -> p b e", b=GB)
                                      for i in range(at, at + 4 * GB * E, GB * E))
        tok_a = act_f[:, 0, 0:PCOLS]
        select_f = act_f[0:E, :, 0:P]
        clsb = h_res[0:NTOK, 0, :]
        onehot_sb = h_mid[0:BUCKETS, 0, 0:NREL]
        table_sb = h_mid[0:BUCKETS, 1, 0:HEADS]

        psS, psT, psC, psD = pb("psS", 2), pb("psT", 1), pb("psC", 2), pb("psD", BANKS)

        consts_loaded = sem("consts_loaded")
        masks_ready = sem("masks_ready")
        masks_made = sem("masks_made")
        piece_loaded = [sem(f"piece_loaded{i}") for i in range(2)]
        piece_hi = sem("piece_hi")
        piece_split = sem("piece_split")
        posb_ready = sem("posb_ready")
        gate_hi = sem("gate_hi")
        gate_split = sem("gate_split")
        select_ready = sem("select_ready")
        pads_zero = sem("pads_zero")
        bias_done = sem("bias_done")
        bias_ready = sem("bias_ready")
        dense_done = sem("dense_done")
        taken = [sem(f"bank{i}_taken") for i in range(BANKS)]
        side_a = sem("side_a")
        qk_lo = sem("qk_lo")
        v_lo = sem("v_lo")
        scores_done, scores_summed = map(sem, ("scores_done", "scores_summed"))
        max_ready, shifted, exp_done, sum_ready, recip_ready, probs_ready = map(
            sem, ("max_ready", "shifted", "exp_done", "sum_ready", "recip_ready", "probs_ready"))
        probsT_done, probsT_hi, probsT_lo = map(sem, ("probsT_done", "probsT_hi", "probsT_lo"))
        ctx_done, ctx_a_ready, ctx_summed, ctx_hi, ctx_lo = map(sem, ("ctx_done", "ctx_a_ready", "ctx_summed", "ctx_hi", "ctx_lo"))
        x_loaded, x_hi, x_split, txt_loaded, mid_loaded, res_loaded, stored = map(
            sem, ("x_loaded", "x_hi", "x_split", "txt_loaded", "mid_loaded", "res_loaded", "stored"))
        tok_gamma, tok_final = map(sem, ("tok_gamma", "tok_final"))
        ln_aggr, ln_var, ln_rstd, ln_shift, ln_out = ({k: sem(f"{nm}_{k}") for k in ln} for nm in (
            "ln_aggr", "ln_var", "ln_rstd", "ln_shift", "ln_out"))
        top2_step, logit_exp, gate_ready = map(sem, ("top2_step", "logit_exp", "gate_ready"))
        tanh_ready, gated, s_hi = map(sem, ("tanh_ready", "gated", "s_hi"))
        s_lo = [sem("s_lo_first"), sem("s_lo_last")]

        def part(w, *index):
            return [t[(slice(None), *index)] for t in w]

        tok_pieces = [(wtok[:, 3 * i:3 * i + 3, :], *part(Wtok, slice(3 * i, 3 * i + 3))) for i in range(2)]
        qkv_pieces = [(wqkv[p], *part(Wqkv, p)) for p in range(PAIRS)]
        wo_pieces = [(wo[:, i:min(i + 3, PAIRS), :], *part(Wo, slice(i, min(i + 3, PAIRS)))) for i in (0, 3, 6)]
        up_pieces = [(wup[t], *part(Wup, t)) for t in range(FT)]
        down_pieces = [(wdown[:, i:i + 2, :], *part(Wdown, slice(i, i + 2))) for i in (0, 2)]
        pieces = tok_pieces + qkv_pieces[:4]
        for a, b in zip(wo_pieces, qkv_pieces[4:7]):
            pieces += [a, b]
        pieces += qkv_pieces[7:] + up_pieces + down_pieces
        qkv_index = [2, 3, 4, 5, 7, 9, 11, 12]
        wo_index = 8
        split_slots = [(-1, n) for n in (1, 2, 3, 4, 9, 11, 12, 14, 15)] + [(0, n) for n in range(SLOTS)]
        split_slot = dict(zip(split_slots, range(2, len(pieces))))

        def staged(i):
            shape = pieces[i][1].shape
            v = stage[:, i % 2, 0:int(np.prod(shape[1:]))]
            if len(shape) == 3:
                return v.rearrange("p (a b) -> p a b", a=shape[1])
            return v.rearrange("p (a b c) -> p a b c", a=shape[1], b=shape[2])

        def images(ap):
            return ap.rearrange("p (b s) -> p b s", b=GB)

        def rows(ap):
            return ap.rearrange("p (b e) -> p b e", b=2)

        block = ctx.enter_context(nc.Block())

        @block.sync
        def _(sp):
            def load_piece(i):
                if i >= 2:
                    sp.wait_ge(piece_split, i - 1)
                sp.dma_start(staged(i), pieces[i][0]).then_inc(piece_loaded[i % 2], 16)

            def group_of(t, first, count):
                return t[first:first + count] if isinstance(first, int) else t[bass.ds(first, count)]

            def moves(g):
                y_jobs = [Job(g, "yback", h, -1) if exists(g, -2) else None for h in range(2)]
                value = {name: v if isinstance(v, int) else sp.snap(v) for name, v in (
                    ("x", g + 1), ("txt", g * GB + GB), ("out0", g * GB - 2 * GB), ("out1", g * GB + (2 - 2 * GB)),
                    ("group", g + 1), ("normal", g * 2 + 2), ("loaded", g * 16), ("moved", g * 16 + 16), ("stored", g * 32 - 32),
                    *((f"y{h}", job.before + 1) for h, job in enumerate(y_jobs) if job))}
                early, late = {-1: (range(0), range(3, 7)), 0: (range(7, 12), range(12, len(pieces)))}.get(
                    g if isinstance(g, int) else None, (range(0), range(0)))
                if exists(g, 1) and not (isinstance(g, int) and g < 0):
                    sp.wait_ge(x_split, value["group"])
                    sp.dma_start(x_raw[:], group_of(xp, value["x"], 1).rearrange("o p k n -> p (o k) n")).then_inc(x_loaded, 16)
                for i in early:
                    load_piece(i)
                for h, job in enumerate(y_jobs):
                    if job:
                        sp.wait_ge(taken[job.bank], value[f"y{h}"])
                        sp.dma_start(group_of(out, value[f"out{h}"], 2).rearrange("b s e -> s b e"),
                                     y[:, 2 * h:2 * h + 2, :]).then_inc(stored, 16)
                if exists(g, -1):
                    at_least(sp, stored, value["stored"])
                    if isinstance(g, int):
                        sp.wait_ge(mid_loaded, value["loaded"])
                    sp.dma_start(h_res[:], h_mid[:]).then_inc(res_loaded, 16)
                if exists(g, 0):
                    if isinstance(g, int) and g == 0:
                        sp.wait_ge(bias_done, 2)
                    at_least(sp, res_loaded, value["loaded"])
                    sp.wait_ge(ln_out["front"], value["normal"])
                    sp.dma_start(h_mid[:], h_new[:]).then_inc(mid_loaded, 16)
                if exists(g, 1):
                    at_least(sp, mid_loaded, value["moved"])
                    sp.dma_start(h_new[NTOK:S, :, :],
                                 group_of(txt, value["txt"], GB).rearrange("b t e -> t b e")).then_inc(txt_loaded, 16)
                for i in late:
                    load_piece(i)

            sp.dma_start(x_raw[:], xp[0:1].rearrange("o p k n -> p (o k) n")).then_inc(x_loaded, 16)
            load_piece(0)
            load_piece(1)
            for dst, src in ((onehot_sb, onehot), (table_sb, table), (posb[:], pos), (h_res[0:1, 0, :], cls),
                             (h_res[1:NTOK, 0, :], btok.partition_broadcast(NPATCH)),
                             (gammab[:], gamma.partition_broadcast(NTOK)),
                             (betab[:], beta.partition_broadcast(NTOK)), (gate_f[:], gatew)):
                sp.dma_start(dst, src).then_inc(consts_loaded, 16)
            load_piece(2)
            for g in range(-1, LOOP_FROM + 1):
                moves(g)
            with sp.Fori(LOOP_FROM + 1, LOOP_TO) as g:
                moves(g)
            for g in range(LOOP_TO, GROUPS + 2):
                moves(g)
            sp.wait_ge(stored, 16 * 2 * GROUPS)

        @block.tensor
        def _(pe):
            def three(out_ap, w, x, first, last):
                pe.matmul(out_ap, w[0], x[0], start=first, stop=False)
                pe.matmul(out_ap, w[0], x[1], start=False, stop=False)
                return pe.matmul(out_ap, w[1], x[0], start=False, stop=last)

            def wait_taken(*jobs, before=None):
                for job in {job.bank: job for job in jobs if not before or job.bank != before.bank}.values():
                    pe.wait_ge(taken[job.bank], job.before + 1)

            def dense(g, kind, i):
                job = Job(g, kind, i)
                ps = psD[:, job.bank, :]
                at_least(pe, taken[job.bank], job.before)
                if kind == "tok":
                    pe.wait_ge(x_split, g + 2)
                    if isinstance(g, int) and g == -1 and i == 0:
                        pe.wait_ge(piece_split, 2)
                    for kt in range(KT):
                        pe.matmul(ps[:, 0:2 * PCOLS], Wtok[0][:, kt, P * i:P * i + P],
                                  x_pix[:, kt, :, :], start=(kt == 0), stop=False)
                        mm = pe.matmul(ps[:, PCOLS:2 * PCOLS], Wtok[1][:, kt, P * i:P * i + P],
                                       x_pix[:, kt, 0, :], start=False, stop=(kt == KT - 1))
                elif kind == "tback":
                    wait_taken(Job(g, "tok", 0), Job(g, "tok", 1), before=job)
                    for b in range(2):
                        for m in range(KD):
                            at = D * b + P * m
                            col = NTOK * (2 * i + b)
                            mm = pe.transpose(ps[0:S, at:at + P], tokT[:, m, col:col + S], ident[:, :])
                elif kind in ("xf", "xb"):
                    pe.wait_ge(ln_out["front" if kind == "xf" else "back"], g * 2 + (4 if kind == "xf" else 0))
                    for b in range(GB):
                        mm = pe.transpose(ps[:, SP * b:SP * b + S], xn[:, b, P * i:P * i + P], ident[0:S, 0:S])
                elif kind in ("q", "k", "vT"):
                    which = ("q", "k", "vT").index(kind)
                    if i == PAIRS and kind == "q":
                        wait_taken(Job(g, "xf", 0), Job(g, "xf", 1), before=job)
                    for k in range(KD):
                        mm = three(ps[:, 0:COLS], [w[:, i % PAIRS, which, k, :] for w in Wqkv],
                                   [x[:, k, :, :] for x in XT], k == 0, k == KD - 1)
                elif kind == "vback":
                    wait_taken(projected(g, "vT", i), before=job)
                    for b in range(GB):
                        mm = pe.transpose(ps[0:S, P * b:P * b + P], vT[:, b, 0:S], ident[:, :])
                elif kind in ("woa", "wob"):
                    first = 0 if kind == "woa" else HALF
                    if isinstance(g, int) and (g, kind, i) == (0, "woa", 0):
                        pe.wait_ge(piece_split, wo_index + 1)
                    for p in range(first, first + HALF):
                        if i == 0:
                            pe.wait_ge(ctx_lo, g * PAIRS + (p + 1 - (0 if kind == "woa" else PAIRS)))
                        mm = three(ps[:, 0:COLS], [w[:, p, P * i:P * i + P] for w in Wo],
                                   [c[:, p, :] for c in ctxT], p == first, p == first + HALF - 1)
                elif kind in ("aback", "yback"):
                    src = "wob" if kind == "aback" else "down"
                    wait_taken(Job(g, src, 0), Job(g, src, 1), before=job)
                    for b in range(2):
                        for m in range(KD):
                            at = D * b + P * m
                            mm = pe.transpose(ps[0:S, at:at + P], aT[:, m, 2 * i + b, 0:S], ident[:, :])
                elif kind == "logit":
                    wait_taken(Job(g, "xb", 0), Job(g, "xb", 1), before=job)
                    for b in range(GB):
                        at = 2 * E * b
                        for k in range(KD):
                            pe.matmul(ps[0:S, at:at + 2 * E], XB[0][:, k, b, 0:S], Wgate[:, k, :, :],
                                      start=(k == 0), stop=False)
                            mm = pe.matmul(ps[0:S, at + E:at + 2 * E], XB[1][:, k, b, 0:S], Wgate[:, k, 0, :],
                                           start=False, stop=(k == KD - 1))
                elif kind in ("u", "v"):
                    for k in range(KD):
                        mm = three(ps[:, 0:COLS], [w[:, i, int(kind == "v"), k, :] for w in Wup],
                                   [x[:, k, :, :] for x in XB], k == 0, k == KD - 1)
                elif kind == "wT":
                    pe.wait_ge(gate_ready, g + 0)
                    for b in range(GB):
                        mm = pe.transpose(ps[0:E, SP * b:SP * b + S], gate[:, b, :], ident[0:S, 0:S])
                elif kind == "mix":
                    wait_taken(Job(g, "wT", 0), before=job)
                    pe.matmul(ps[:, 0:COLS], select[:, i, :], wT[0][:, :, :], start=True, stop=False)
                    mm = pe.matmul(ps[:, 0:COLS], select[:, i, :], wT[1][:, :, :], start=False, stop=True)
                elif kind == "down":
                    for t in range(FT):
                        if i == 0:
                            if t == 0:
                                pe.wait_ge(s_lo[0], g + 0)
                            else:
                                pe.wait_ge(s_lo[1], g * (FT - 1) + (t - (FT - 1)))
                        mm = three(ps[:, 0:COLS], [w[:, t, P * i:P * i + P] for w in Wdown],
                                   [x[:, t, :] for x in sT], t == 0, t == FT - 1)
                mm.then_inc(dense_done, 1)

            def scores(g, m):
                p = m // 2
                if m % 2 == 0:
                    pe.wait_ge(qk_lo, g * 2 * PAIRS + (2 * p + 2))
                at_least(pe, scores_summed, g * SLOTS + m)
                for b in range(2):
                    img = 2 * (m % 2) + b
                    for h in range(2):
                        r, at = slice(DH * h, DH * h + DH), SP * b
                        mm = three(psS[0:S, h, at:at + SP], [q[r, img, 0:S] for q in Q[p % 2]],
                                   [k[r, img, :] for k in K[p % 2]], True, True)
                mm.then_inc(scores_done, 1)

            def probs_transposed(g, m):
                pe.wait_ge(probs_ready, g * SLOTS + (m + 1))
                at_least(pe, probsT_lo, g * SLOTS + m)
                for b in range(2):
                    for h in range(2):
                        at = SP * (2 * b + h)
                        mm = pe.transpose(psT[0:S, 0, at:at + S], prob[:, m % 4, 2 * h + b, :], ident[0:S, 0:S])
                mm.then_inc(probsT_done, 1)

            def context(g, m):
                p = m // 2
                if m % 2 == 0:
                    pe.wait_ge(v_lo, g * PAIRS + (p + 1))
                pe.wait_ge(probsT_lo, g * SLOTS + (m + 1))
                at_least(pe, ctx_summed, g * SLOTS + m)
                for b in range(2):
                    img = 2 * (m % 2) + b
                    pe.matmul(psC[:, b, 0:4 * SP], V[p % 2][0][:, img, :], PT[m % 2][:, b, :, :, :],
                              start=True, stop=False)
                    mm = pe.matmul(psC[:, b, 2 * SP:4 * SP], V[p % 2][1][:, img, :], PT[m % 2][:, b, 0, :, :],
                                   start=False, stop=True)
                mm.then_inc(ctx_done, 1)

            def position_bias(keys):
                for k in keys:
                    at = HEADS * (k % 32)
                    mm = pe.matmul((psS, psT, psC)[k // 32][0:S, 0, at:at + HEADS],
                                   onehot_sb[:, S - 1 - k:2 * S - 1 - k], table_sb, start=True, stop=True)
                mm.then_inc(bias_done, 1)

            def body(g):
                static = isinstance(g, int)
                for n in range(SLOTS):
                    first, second, third, proj, fourth = slot_jobs(g, n)
                    if static and (g, n) == (-1, 6):
                        position_bias(range(FIRST_KEYS, S))
                    if static and (g, n) == (-1, 13):
                        pe.wait_ge(bias_ready, 1)
                    if alive(g, n + 3):
                        scores(g, n + 3)
                    for kind, i in first:
                        dense(g, kind, i)
                    if alive(g, n):
                        probs_transposed(g, n)
                    for kind, i in second:
                        dense(g, kind, i)
                    if alive(g, n - 1):
                        context(g, n - 1)
                    for kind, i in third:
                        dense(g, kind, i)
                    for kind, i in proj:
                        if static and g < 1 and kind == "q" and PAIRS * g + i < PAIRS:
                            pe.wait_ge(piece_split, qkv_index[i % PAIRS] + 1)
                        dense(g, kind, i)
                    for kind, i in fourth:
                        dense(g, kind, i)

            pe.wait_ge(masks_made, 3)
            pe.wait_ge(pads_zero, 1)
            pe.wait_ge(consts_loaded, 16 * 8)
            position_bias(range(FIRST_KEYS))
            body(-1)
            body(0)
            pe.wait_ge(piece_split, len(pieces))
            pe.wait_ge(gate_split, 1)
            pe.wait_ge(select_ready, 1)
            with pe.Fori(LOOP_FROM, LOOP_TO) as g:
                body(g)
            body(GROUPS - 1)
            body(GROUPS)

        @block.scalar
        def _(act):
            def piece(i):
                act.wait_ge(piece_loaded[i % 2], 16 * (i // 2 + 1))
                act.copy(pieces[i][1], staged(i)).then_inc(piece_hi, 1)

            def dense(g, kind, i):
                if kind in ("tback", "wob", "aback", "yback", "mix"):
                    return
                job = Job(g, kind, i)
                ps = psD[:, job.bank, :]
                act.wait_ge(dense_done, job.number + 1)
                if kind == "tok":
                    if i == 1:
                        last = Job(g, "tok", 0)
                        act.wait_ge(taken[last.bank], last.before + 1)
                    act.copy(tok_a[:], ps[:, 0:PCOLS]).then_inc(side_a, 1)
                elif kind in ("xf", "xb"):
                    act.copy((XT if kind == "xf" else XB)[0][:, i, :, 0:S],
                             images(ps[:, 0:COLS])[:, :, 0:S]).then_inc(side_a, 1)
                elif kind in ("q", "k"):
                    full, X = (q_full, Q[i % 2]) if kind == "q" else (k_full, K[i % 2])
                    at_least(act, qk_lo, g * 2 * PAIRS + (2 * i - (kind == "q")))
                    act.copy(full[:, :, :], images(ps[:, 0:COLS]))
                    at_least(act, scores_done, g * SLOTS + (2 * i - 2))
                    act.copy(X[0][:, :, :], images(ps[:, 0:COLS])).then_inc(taken[job.bank], 1)
                elif kind == "vT":
                    act.copy(vT[:, :, :], images(ps[:, 0:COLS])).then_inc(taken[job.bank], 1)
                elif kind == "vback":
                    at_least(act, v_lo, g * PAIRS + i)
                    act.copy(v_full[:, :, :], images(ps[0:S, :]))
                    at_least(act, ctx_done, g * SLOTS + (2 * i - 2))
                    act.copy(V[i % 2][0][:, :, :], images(ps[0:S, :])).then_inc(taken[job.bank], 1)
                elif kind == "woa":
                    if isinstance(g, int) and g == 0 and i == 0:
                        act.wait_ge(piece_split, len(pieces))
                    act.copy(wo_part[:, i, :], ps[:, 0:COLS]).then_inc(taken[job.bank], 1)
                elif kind == "down":
                    act.copy(aT[:, i, :, :], images(ps[:, 0:COLS])).then_inc(taken[job.bank], 1)
                elif kind == "logit":
                    act.copy(logit_a[:], images(ps[0:S, 0:2 * E * GB])[:, :, 0:E]).then_inc(side_a, 1)
                elif kind == "u":
                    if i > 0:
                        last = Job(g, "u", i - 1)
                        act.wait_ge(taken[last.bank], last.before + 1)
                    act.activation(th[:], ps[:, 0:COLS], ACT.Tanh, scale=0.5).then_inc(tanh_ready, 1)
                elif kind == "v":
                    if i >= 2:
                        act.wait_ge(gated, g * FT + (i - 1 - FT))
                    act.copy(ffn_v[:, i % 2, :], ps[:, 0:COLS]).then_inc(taken[job.bank], 1)
                elif kind == "wT":
                    act.copy(wT[0][:, :, 0:S], images(ps[0:E, 0:COLS])[:, :, 0:S]).then_inc(side_a, 1)

            def normalise(g, kind, off, src):
                act.wait_ge(ln_shift[kind], g + (off + 1))
                for b in range(2):
                    last = act.activation(xn[:, b, :], src[:, b, :], ACT.Identity,
                                          bias=ln[kind]["nm"][:, b:b + 1], scale=ln[kind]["rs"][:, b:b + 1])
                last.then_inc(ln_out[kind], 1)

            def weighted_hi(g, tiles):
                for t in tiles:
                    job = Job(g, "mix", t)
                    act.wait_ge(taken[job.bank], job.before + 1)
                    act.copy(sT[0][:, t, :], act_f[:, t, :]).then_inc(s_hi, 1)

            def body(g):
                static = isinstance(g, int)
                for n in range(SLOTS):
                    first, second, third, proj, fourth = slot_jobs(g, n)
                    if n == 13 and exists(g, -1):
                        weighted_hi(g, range(FT))
                    for kind, i in first:
                        dense(g, kind, i)
                    if alive(g, n):
                        m = n
                        act.wait_ge(probsT_done, g * SLOTS + (m + 1))
                        at_least(act, ctx_done, g * SLOTS + (m - 1))
                        act.copy(PT[m % 2][:, :, 0, :, 0:S],
                                 psT[0:S, 0, 0:4 * SP].rearrange("p (b h c) -> p b h c", b=2, h=2)[:, :, :, 0:S])\
                           .then_inc(probsT_hi, 1)
                    if alive(g, n + 2):
                        m = n + 2
                        act.wait_ge(shifted, g * SLOTS + (m + 1))
                        act.activation(prob[:, m % 4, :, :], prob[:, m % 4, :, :], ACT.Exp, scale=SCALE).then_inc(exp_done, 1)
                    for kind, i in second:
                        dense(g, kind, i)
                    if n == (7 if last_body(g) else TOP2_EXP) and exists(g, -1):
                        act.wait_ge(top2_step, g * TOP2_STEPS + (5 - TOP2_STEPS))
                        act.activation(gate[:], gate[:], ACT.Exp).then_inc(logit_exp, 1)
                    if alive(g, n - 1):
                        m = n - 1
                        act.wait_ge(ctx_done, g * SLOTS + (m + 1))
                        at_least(act, ctx_summed, g * SLOTS + m)
                        act.copy(ctx_a[:, :, :], psC[:, :, 0:2 * SP]).then_inc(ctx_a_ready, 1)
                    if n == 4 and exists(g, -1):
                        normalise(g, "back", -1, h_res)
                    if n == 10 and exists(g, 1):
                        normalise(g, "front", 1, h_new)
                    for kind, i in third:
                        dense(g, kind, i)
                    for kind, i in proj:
                        dense(g, kind, i)
                    for kind, i in fourth:
                        dense(g, kind, i)
                    if n % 2 == 0 and alive(g, n - 1):
                        m = n - 1
                        p = (m // 2) % PAIRS
                        act.wait_ge(ctx_summed, g * SLOTS + (m + 1))
                        act.copy(ctxT[0][:, p, :], ctx_f[:, p % 2, :, :].rearrange("p b s -> p (b s)")).then_inc(ctx_hi, 1)
                    if n == 1 and exists(g, 1):
                        act.wait_ge(x_loaded, g * 16 + 32)
                        act.copy(x_pix[:, :, 0, :], x_raw[:, :, :]).then_inc(x_hi, 1)
                    if static and (g, n) in split_slot:
                        piece(split_slot[g, n])

            piece(0)
            piece(1)
            act.wait_ge(masks_made, 3)
            act.copy(select[:], select_f).then_inc(select_ready, 1)
            act.wait_ge(pads_zero, 1)
            body(-1)
            act.wait_ge(consts_loaded, 16 * 8)
            act.copy(Wgate[:, :, 0, :], gate_f[:, :, :]).then_inc(gate_hi, 1)
            body(0)
            with act.Fori(LOOP_FROM, LOOP_TO) as g:
                body(g)
            body(GROUPS - 1)
            body(GROUPS)

        @block.vector
        def _(dve):
            def lo_part(lo, full, hi):
                return dve.tensor_tensor(lo, full, hi.bitcast(F32), ALU.subtract)

            def piece(i):
                dve.wait_ge(piece_hi, i + 1)
                lo_part(pieces[i][2], staged(i), pieces[i][1]).then_inc(piece_split, 1)

            def dense(g, kind, i):
                if kind in ("q", "k", "vT", "vback", "woa", "v", "down"):
                    return
                job = Job(g, kind, i)
                ps = psD[:, job.bank, :]
                free = taken[job.bank]
                if kind in SIDED:
                    dve.wait_ge(side_a, job.sided)
                else:
                    dve.wait_ge(dense_done, job.number + 1)
                if kind == "tok":
                    dve.tensor_tensor(images(tokT[:, i, 0:GB * NTOK])[:, :, 1:NTOK], images(ps[:, PCOLS:2 * PCOLS]), images(tok_a[:]),
                                      ALU.add).then_inc(free, 1)
                elif kind == "tback":
                    at_least(dve, mid_loaded, g * 16 + 16)
                    dve.tensor_tensor(h_new[0:NTOK, 2 * i:2 * i + 2, :], rows(ps[0:NTOK, :]),
                                      posb[:].unsqueeze(1).to_broadcast((NTOK, 2, D)), ALU.add).then_inc(free, 1)
                elif kind in ("xf", "xb"):
                    X = XT if kind == "xf" else XB
                    lo_part(X[1][:, i, :, 0:S], images(ps[:, 0:COLS])[:, :, 0:S], X[0][:, i, :, 0:S]).then_inc(free, 1)
                elif kind == "wob":
                    first = Job(g, "woa", i, -1)
                    dve.wait_ge(taken[first.bank], first.before + 1)
                    dve.tensor_tensor(aT[:, i, :, :], images(ps[:, 0:COLS]), images(wo_part[:, i, :]),
                                      ALU.add).then_inc(free, 1)
                elif kind == "aback":
                    dve.wait_ge(res_loaded, g * 16)
                    res = h_res[:, 2 * i:2 * i + 2, :]
                    dve.tensor_tensor(res, rows(ps[0:S, :]), res, ALU.add).then_inc(free, 1)
                elif kind == "yback":
                    dve.tensor_tensor(y[:, 2 * i:2 * i + 2, :], rows(ps[0:S, :]), h_res[:, 2 * i:2 * i + 2, :],
                                      ALU.add).then_inc(free, 1)
                elif kind == "logit":
                    dve.tensor_tensor(logit[:], images(ps[0:S, 0:2 * E * GB])[:, :, E:2 * E], logit_a[:],
                                      ALU.add).then_inc(free, 1)
                elif kind == "u":
                    dve.wait_ge(tanh_ready, g * FT + (i + 1 - FT))
                    dve.scalar_tensor_tensor(act_f[:, i, :], th[:], 1.0, ps[:, 0:COLS], ALU.add, ALU.mult).then_inc(free, 1)
                elif kind == "wT":
                    lo_part(wT[1][:, :, 0:S], images(ps[0:E, 0:COLS])[:, :, 0:S], wT[0][:, :, 0:S]).then_inc(free, 1)
                elif kind == "mix":
                    dve.wait_ge(gated, g * FT + (i + 1 - FT))
                    dve.tensor_tensor(act_f[:, i, :], ps[:, 0:COLS], act_f[:, i, :], ALU.mult).then_inc(free, 1)

            def row_stats(kind, src, n_rows, pair):
                for b in (2 * pair, 2 * pair + 1):
                    dve.bn_stats(ln[kind]["st"][0:n_rows, b, :], src[0:n_rows, b, :])

            def variance(g, kind, off, n_rows):
                t = ln[kind]
                dve.drain()
                for b in range(GB):
                    last = dve.bn_aggr(t["mv"][0:n_rows, b, :], t["st"][0:n_rows, b, :])
                last.then_inc(ln_aggr[kind], 1)
                dve.wait_ge(ln_aggr[kind], g + (off + 1))
                dve.tensor_scalar(t["ve"][0:n_rows, :], t["mv"][0:n_rows, :, 1], EPS, None, ALU.add).then_inc(ln_var[kind], 1)

            def shift_of(g, kind, off):
                t = ln[kind]
                dve.wait_ge(ln_rstd[kind], g + (off + 1))
                dve.scalar_tensor_tensor(t["nm"][:, :], t["mv"][:, :, 0], -1.0, t["rs"][:, :],
                                         ALU.mult, ALU.mult).then_inc(ln_shift[kind], 1)

            def normalise(g, kind, off, src):
                t = ln[kind]
                for b in range(2, GB):
                    last = dve.tensor_scalar(xn[:, b, :], src[:, b, :], t["mv"][:, b, 0:1], t["rs"][:, b:b + 1],
                                             ALU.subtract, ALU.mult)
                last.then_inc(ln_out[kind], 1)

            def top2(g, part_no):
                def step(k):
                    dve.wait_ge(top2_step, g * TOP2_STEPS + (k - TOP2_STEPS))

                four = (S, GB, E, E)
                if part_no == 0:
                    job = Job(g, "logit", 0)
                    dve.wait_ge(taken[job.bank], job.before + 1)
                    of_e = logit[:].unsqueeze(3).to_broadcast(four)
                    of_other = logit[:].unsqueeze(2).to_broadcast(four)
                    dve.tensor_tensor(above[:], of_other, of_e, ALU.is_gt).then_inc(top2_step, 1)
                    dve.tensor_tensor(same[:], of_other, of_e, ALU.is_equal).then_inc(top2_step, 1)
                    dve.tensor_reduce(top[:], logit[:], AX.X, ALU.max).then_inc(top2_step, 1)
                elif part_no == 1:
                    step(3)
                    dve.tensor_tensor(gate[:], logit[:], top[:].unsqueeze(2).to_broadcast((S, GB, E)),
                                      ALU.subtract).then_inc(top2_step, 1)
                    dve.tensor_tensor(same[:].rearrange("p b e f -> p b (e f)"), same[:].rearrange("p b e f -> p b (e f)"),
                                      earlier[0:S].rearrange("p e f -> p (e f)").unsqueeze(1).to_broadcast((S, GB, E * E)),
                                      ALU.mult).then_inc(top2_step, 1)
                elif part_no == 2:
                    step(5)
                    dve.tensor_tensor(above[:], above[:], same[:], ALU.add).then_inc(top2_step, 1)
                elif part_no == 3:
                    step(6)
                    dve.tensor_reduce(rank[:], above[:], AX.X, ALU.add).then_inc(top2_step, 1)
                elif part_no == 4:
                    step(7)
                    dve.tensor_scalar(keep[:], rank[:], 1.5, None, ALU.is_lt).then_inc(top2_step, 1)
                    step(8)
                    dve.wait_ge(logit_exp, g + 0)
                    dve.tensor_tensor(gate[:], gate[:], keep[:], ALU.mult).then_inc(top2_step, 1)
                else:
                    step(9)
                    dve.tensor_reduce(wsum[:], gate[:], AX.X, ALU.add).then_inc(top2_step, 1)
                    step(10)
                    dve.reciprocal(wrec[:], wsum[:]).then_inc(top2_step, 1)
                    step(11)
                    dve.scalar_tensor_tensor(gate[:], gate[:], 0.5, wrec[:].unsqueeze(2).to_broadcast((S, GB, E)),
                                             ALU.mult, ALU.mult).then_inc(gate_ready, 1)

            def top2_parts(g):
                if last_body(g):
                    return {(6, 2): (0, 1, 2, 3), (7, 2): (4, 5)}
                return {(8, 1): (0,), (10, 2): (1,), (11, 0): (2,), (11, 1): (3,), (12, 0): (4, 5)}

            def back_rows(g, at):
                if at == (2, 2):
                    last = Job(g, "aback", 1)
                    dve.wait_ge(taken[last.bank], last.before + 1)
                    row_stats("back", h_res, S, 0)
                elif at == (3, 0):
                    row_stats("back", h_res, S, 1)
                elif at == (3, 1):
                    variance(g, "back", -1, S)
                elif at == (4, 0):
                    shift_of(g, "back", -1)
                elif at == (4, 1):
                    normalise(g, "back", -1, h_res)
                elif at in top2_parts(g):
                    for part_no in top2_parts(g)[at]:
                        top2(g, part_no)
                elif at == (13, 2):
                    for t in range(1, FT):
                        dve.wait_ge(s_hi, g * FT + (t + 1 - FT))
                        lo_part(sT[1][:, t, :], act_f[:, t, :], sT[0][:, t, :]).then_inc(s_lo[1], 1)

            def front_rows(g, at):
                t = ln["tok"]
                if at == (5, 2):
                    last = Job(g, "tback", 1)
                    dve.wait_ge(taken[last.bank], last.before + 1)
                    row_stats("tok", h_new, NTOK, 0)
                elif at == (6, 0):
                    row_stats("tok", h_new, NTOK, 1)
                elif at == (6, 1):
                    variance(g, "tok", 1, NTOK)
                elif at in ((6, 2), (7, 0)):
                    for b in (0, 1) if at == (6, 2) else (2, 3):
                        last = dve.scalar_tensor_tensor(h_new[0:NTOK, b, :], h_new[0:NTOK, b, :],
                                                        t["mv"][0:NTOK, b, 0:1], gammab[:], ALU.subtract, ALU.mult)
                    last.then_inc(tok_gamma, 1)
                elif at in ((7, 2), (8, 0)):
                    if at == (7, 2):
                        dve.wait_ge(ln_rstd["tok"], g + 2)
                        dve.wait_ge(tok_gamma, g * 2 + 4)
                    for b in (0, 1) if at == (7, 2) else (2, 3):
                        last = dve.scalar_tensor_tensor(h_new[0:NTOK, b, :], h_new[0:NTOK, b, :],
                                                        t["rs"][0:NTOK, b:b + 1], betab[:], ALU.mult, ALU.add)
                    last.then_inc(tok_final, 1)
                elif at == (8, 2):
                    dve.wait_ge(tok_final, g * 2 + 4)
                    dve.wait_ge(txt_loaded, g * 16 + 32)
                    row_stats("front", h_new, S, 0)
                elif at == (9, 0):
                    row_stats("front", h_new, S, 1)
                elif at == (9, 1):
                    variance(g, "front", 1, S)
                elif at == (10, 0):
                    shift_of(g, "front", 1)
                elif at == (10, 1):
                    normalise(g, "front", 1, h_new)

            def position_bias():
                dve.wait_ge(bias_done, 2)
                for c in range(3):
                    lo, hi = 32 * c, min(32 * c + 32, S)
                    last = dve.tensor_scalar(bias[:, :, lo:hi], (psS, psT, psC)[c][0:S, 0, 0:HEADS * (hi - lo)]
                                             .rearrange("p (k h) -> p h k", h=HEADS), 1 / SCALE, None, ALU.mult)
                last.then_inc(bias_ready, 1)

            def rows_work(g, at):
                if exists(g, -1):
                    back_rows(g, at)
                if exists(g, 1):
                    front_rows(g, at)

            def body(g):
                static = isinstance(g, int)
                for n in range(SLOTS):
                    first, second, third, proj, fourth = slot_jobs(g, n)
                    if alive(g, n + 1):
                        m = n + 1
                        dve.wait_ge(sum_ready, g * SLOTS + (m + 1))
                        dve.reciprocal(rc[:, m % 4, :], sm[:, m % 4, :]).then_inc(recip_ready, 1)
                    if alive(g, n + 3):
                        m = n + 3
                        p = (m // 2) % PAIRS
                        dve.wait_ge(scores_done, g * SLOTS + (m + 1))
                        dve.tensor_tensor(
                            prob[:, m % 4, :, :].rearrange("p (h b) k -> p h b k", h=2),
                            psS[0:S, :, 0:2 * SP].rearrange("p h (b k) -> p h b k", b=2)[:, :, :, 0:S],
                            bias[:, 2 * p:2 * p + 2, :].unsqueeze(2).to_broadcast((S, 2, 2, S)),
                            ALU.add).then_inc(scores_summed, 1)
                    rows_work(g, (n, 0))
                    if alive(g, n + 3):
                        m = n + 3
                        dve.wait_ge(scores_summed, g * SLOTS + (m + 1))
                        dve.tensor_reduce(mx[:, m % 4, :], prob[:, m % 4, :, :], AX.X, ALU.max).then_inc(max_ready, 1)
                    for kind, i in first:
                        dense(g, kind, i)
                    if alive(g, n):
                        m = n
                        dve.wait_ge(probsT_hi, g * SLOTS + (m + 1))
                        lo_part(PT[m % 2][:, :, 1, :, 0:S],
                                psT[0:S, 0, 0:4 * SP].rearrange("p (b h c) -> p b h c", b=2, h=2)[:, :, :, 0:S],
                                PT[m % 2][:, :, 0, :, 0:S]).then_inc(probsT_lo, 1)
                    rows_work(g, (n, 1))
                    for kind, i in second:
                        dense(g, kind, i)
                    if alive(g, n - 1):
                        m = n - 1
                        p, img = (m // 2) % PAIRS, 2 * (m % 2)
                        dve.wait_ge(ctx_a_ready, g * SLOTS + (m + 1))
                        at_least(dve, ctx_lo, g * PAIRS + (m // 2 - 1))
                        for h in range(2):
                            r = slice(DH * h, DH * h + DH)
                            last = dve.tensor_tensor(ctx_f[r, p % 2, img:img + 2, :],
                                                     psC[r, :, SP * (2 + h):SP * (3 + h)],
                                                     ctx_a[r, :, SP * h:SP * h + SP], ALU.add)
                        last.then_inc(ctx_summed, 1)
                    for kind, i in third:
                        dense(g, kind, i)
                    for kind, i in proj:
                        dense(g, kind, i)
                    for kind, i in fourth:
                        dense(g, kind, i)
                    rows_work(g, (n, 2))
                    if alive(g, n + 2):
                        m = n + 2
                        dve.wait_ge(exp_done, g * SLOTS + (m + 1))
                        dve.tensor_reduce(sm[:, m % 4, :], prob[:, m % 4, :, :], AX.X, ALU.add).then_inc(sum_ready, 1)
                    if static and (g, n) == (-1, 11):
                        position_bias()
                    if static and (g, n) in split_slot:
                        piece(split_slot[g, n])

            piece(0)
            piece(1)
            dve.wait_ge(consts_loaded, 16 * 8)
            dve.tensor_tensor(posb[:], posb[:], clsb, ALU.add).then_inc(posb_ready, 1)
            dve.wait_ge(posb_ready, 1)
            dve.wait_ge(pads_zero, 1)
            dve.wait_ge(masks_made, 3)
            body(-1)
            body(0)
            dve.wait_ge(gate_hi, 1)
            lo_part(Wgate[:, :, 1, :], gate_f[:, :, :], Wgate[:, :, 0, :]).then_inc(gate_split, 1)
            with dve.Fori(LOOP_FROM, LOOP_TO) as g:
                body(g)
            body(GROUPS - 1)
            body(GROUPS)

        @block.gpsimd
        def _(pool):
            def power(g, kind, off, n_rows):
                t = ln[kind]
                pool.wait_ge(ln_var[kind], g + (off + 1))
                pool.tensor_tensor(t["rs"][0:n_rows, :], t["ve"][0:n_rows, :], minus_half[0:n_rows, :],
                                   ALU.pow).then_inc(ln_rstd[kind], 1)

            def split(g, n, kind, i):
                job = Job(g, kind, i, 0 if n else -1)
                pool.wait_ge(taken[job.bank], job.before + 1)
                full, (hi, lo), ready = {"q": (q_full, Q[i % 2], qk_lo), "k": (k_full, K[i % 2], qk_lo),
                                         "vback": (v_full, V[i % 2], v_lo)}[kind]
                pool.tensor_tensor(lo[:], full[:], hi[:].bitcast(F32), ALU.subtract).then_inc(ready, 1)

            def body(g):
                for n in range(SLOTS):
                    if alive(g, n + 2):
                        m = n + 2
                        pool.wait_ge(max_ready, g * SLOTS + (m + 1))
                        pr = prob[:, m % 4, :, :]
                        pool.tensor_tensor(pr, pr, mx[:, m % 4, :].unsqueeze(2).to_broadcast((S, 4, S)),
                                           ALU.subtract).then_inc(shifted, 1)
                    if n == 4 and exists(g, -1):
                        power(g, "back", -1, S)
                    if n == 7 and exists(g, 1):
                        power(g, "tok", 1, NTOK)
                    if n == 10 and exists(g, 1):
                        power(g, "front", 1, S)
                    if n % 2 == 1 and alive(g, n - 2):
                        m = n - 2
                        p = (m // 2) % PAIRS
                        pool.wait_ge(ctx_hi, g * PAIRS + (m // 2 + 1))
                        pool.tensor_tensor(ctxT[1][:, p, :], ctx_f[:, p % 2, :, :].rearrange("p b s -> p (b s)"),
                                           ctxT[0][:, p, :].bitcast(F32), ALU.subtract).then_inc(ctx_lo, 1)
                    just_done = slot_jobs(g, n - 1)[3] if n else slot_jobs(g - 1 if isinstance(g, int) else g, SLOTS - 1)[3]
                    for kind, i in just_done:
                        if kind in ("q", "k"):
                            split(g, n, kind, i)
                    if alive(g, n + 1):
                        m = n + 1
                        pool.wait_ge(recip_ready, g * SLOTS + (m + 1))
                        pr = prob[:, m % 4, :, :]
                        pool.tensor_tensor(pr, pr, rc[:, m % 4, :].unsqueeze(2).to_broadcast((S, 4, S)),
                                           ALU.mult).then_inc(probs_ready, 1)
                    if n == 13 and exists(g, -1):
                        pool.wait_ge(s_hi, g * FT + (1 - FT))
                        pool.tensor_tensor(sT[1][:, 0, :], act_f[:, 0, :], sT[0][:, 0, :].bitcast(F32),
                                           ALU.subtract).then_inc(s_lo[0], 1)
                    if n in (7, 8, 9, 11) and exists(g, -1):
                        t = (7, 8, 9, 11).index(n)
                        for kind in ("u", "v"):
                            job = Job(g, kind, t)
                            pool.wait_ge(taken[job.bank], job.before + 1)
                        pool.tensor_tensor(act_f[:, t, :], act_f[:, t, :], ffn_v[:, t % 2, :], ALU.mult).then_inc(gated, 1)
                    for kind, i in just_done:
                        if kind == "vback":
                            split(g, n, kind, i)
                    if n == 2 and exists(g, 1):
                        pool.wait_ge(x_hi, g + 2)
                        pool.tensor_tensor(x_pix[:, :, 1, :], x_raw[:, :, :], x_pix[:, :, 0, :].bitcast(F32),
                                           ALU.subtract).then_inc(x_split, 1)

            pool.memset(ident[:], 0.0).then_inc(masks_ready, 1)
            pool.memset(select_f, 0.0).then_inc(masks_ready, 1)
            pool.memset(earlier[:], 1.0).then_inc(masks_ready, 1)
            pool.memset(minus_half[:], -0.5)
            for t in (*XT, *XB, *wT, *PT, tokT):
                last = pool.memset(t[:] if t is tokT else t[:].bitcast(F32), 0.0)
            last.then_inc(pads_zero, 1)
            pool.wait_ge(masks_ready, 3)
            pool.affine_select(out=ident[:], in_=ident[:], compare_op=ALU.not_equal, fill=1.0, base=0,
                               pattern=[[-1, P]], channel_multiplier=1).then_inc(masks_made, 1)
            sel = select_f.rearrange("e t (a r) -> e t a r", a=2)
            pool.affine_select(out=sel, in_=sel, compare_op=ALU.not_equal, fill=1.0, base=0,
                               pattern=[[-2, FT], [-1, 2], [0, R]], channel_multiplier=1).then_inc(masks_made, 1)
            pool.affine_select(out=earlier[:], in_=earlier[:], compare_op=ALU.is_gt, fill=0.0, base=0,
                               pattern=[[1, E], [-1, E]], channel_multiplier=0).then_inc(masks_made, 1)
            body(-1)
            body(0)
            with pool.Fori(LOOP_FROM, LOOP_TO) as g:
                body(g)
            body(GROUPS - 1)
            body(GROUPS)


def bucket_one_hot():
    table = np.zeros((BUCKETS, NREL), np.float32)
    for i in range(NREL):
        rel = S - 1 - i
        dist = abs(rel)
        far = sum(dist >= edge for edge in (8, 12, 16, 23, 32, 46, 64))
        table[(dist if dist < 8 else 7 + far) + (16 if rel > 0 else 0), i] = 1.0
    return table


def kernel(**inputs):
    import concourse.bacc as bacc
    from concourse.bass_utils import run_bass_kernel_spmd

    a = {k: np.asarray(v) for k, v in inputs.items()}
    x = a["x"].reshape(GROUPS, GB, CHAN, SIDE, PATCH, SIDE, PATCH).transpose(0, 2, 4, 6, 1, 3, 5)
    x = x.reshape(GROUPS, KT, P, PCOLS).transpose(0, 2, 1, 3)
    qkv = np.stack([a["L0_attn_Wq"], a["L0_attn_Wk"], a["L0_attn_Wv"]]).reshape(3, KD, P, PAIRS, P)
    up = np.stack([a["L0_ffn_Wu"], a["L0_ffn_Wv"]]).reshape(2, FT, 2, KD, P, R)
    arrays = {
        "xp": x,
        "txt": a["txt"],
        "wtok": a["L0_tok_W"].reshape(KT, P, D).transpose(1, 0, 2),
        "btok": a["L0_tok_b"],
        "cls": a["L0_tok_cls_token"].reshape(1, D),
        "pos": a["L0_tok_pos_embedding"].reshape(NTOK, D),
        "gamma": a["L0_tok_gamma"],
        "beta": a["L0_tok_beta"],
        "wqkv": qkv.transpose(3, 2, 0, 1, 4),
        "wo": a["L0_attn_Wo"].reshape(PAIRS, P, D).transpose(1, 0, 2),
        "table": a["L0_attn_rel_bias_table"],
        "gatew": a["L0_ffn_gate_w"].reshape(KD, P, E).transpose(1, 0, 2),
        "wup": up.transpose(1, 4, 0, 3, 2, 5).reshape(FT, P, 2, KD, P),
        "wdown": a["L0_ffn_Wo"].reshape(FT, P, D).transpose(1, 0, 2),
        "onehot": bucket_one_hot(),
    }
    arrays = {k: np.ascontiguousarray(v) for k, v in arrays.items()}
    nc = bacc.Bacc("TRN2", target_bir_lowering=False, num_devices=1, dynamic_dma_scratch_size=1024)
    args = [nc.dram_tensor(k, v.shape, F32, kind="ExternalInput").ap() for k, v in arrays.items()]
    out = nc.dram_tensor("out", (BATCH, S, D), F32, kind="ExternalOutput").ap()
    build(nc, *args, out)
    r = run_bass_kernel_spmd(nc, [arrays], core_ids=[0])
    return r.results[0]["out"]
```
